# Optimizing a Trainium2 kernel written in Bass

```python
import numpy as np
import jax
import jax.numpy as jnp

def _softmax(x, axis=-1):
    return jax.nn.softmax(x, axis=axis)

def _gelu(x):
    return jax.nn.gelu(x, approximate=True)

def _silu(x):
    return jax.nn.silu(x)

def _sigmoid(x):
    return jax.nn.sigmoid(x)

def _layernorm(x, axis=-1, eps=1e-05):
    m = jnp.mean(x, axis=axis, keepdims=True)
    v = jnp.var(x, axis=axis, keepdims=True)
    return (x - m) / jnp.sqrt(v + eps)

def _scatter_add(tgt, idx, src, axis=0):
    return tgt.at[idx].add(src)

def _segment_sum(src, seg, n):
    return jax.ops.segment_sum(src, seg, n)
kernel_name = 'mk_macaron_d2_jaxref_r8_199578'

def setup_inputs(seed: int=0):
    np.random.seed(seed)
    _w = jnp.asarray

    def _L0_attn_setup():
        import jax, jax.numpy as jnp
        import numpy as np
        NUM_HEADS = 16
        LN_EPS = 1e-05
        key = jax.random.key(seed)
        ks = jax.random.split(key, 5)
        B, S, E = (4, 128, 128)
        x = jax.random.normal(ks[0], (B, S, E), dtype=jnp.float32)
        Wq = jax.random.normal(ks[1], (E, E), dtype=jnp.float32) * E ** (-0.5)
        Wk = jax.random.normal(ks[2], (E, E), dtype=jnp.float32) * E ** (-0.5)
        Wv = jax.random.normal(ks[3], (E, E), dtype=jnp.float32) * E ** (-0.5)
        Wo = jax.random.normal(ks[4], (E, E), dtype=jnp.float32) * E ** (-0.5)
        gamma = jnp.ones((E,), dtype=jnp.float32)
        beta = jnp.zeros((E,), dtype=jnp.float32)
        return {'x': x, 'Wq': Wq, 'Wk': Wk, 'Wv': Wv, 'Wo': Wo, 'gamma': gamma, 'beta': beta}
    _L0_attn_in = _L0_attn_setup()

    def _L0_ffn_setup():
        import jax, jax.numpy as jnp
        import numpy as np
        D_MODEL, D_FF, RANK = (128, 512, 32)
        B, S = (4, 512)
        key = jax.random.key(seed)
        ks = jax.random.split(key, 7)
        return {'x': jax.random.normal(ks[0], (B, S, D_MODEL), dtype=jnp.float32), 'U1': jax.random.normal(ks[1], (D_MODEL, RANK), dtype=jnp.float32) * 0.02, 'V1': jax.random.normal(ks[2], (RANK, D_FF), dtype=jnp.float32) * 0.02, 'b1': jnp.zeros((D_FF,), dtype=jnp.float32), 'U2': jax.random.normal(ks[3], (D_FF, RANK), dtype=jnp.float32) * 0.02, 'V2': jax.random.normal(ks[4], (RANK, D_MODEL), dtype=jnp.float32) * 0.02, 'b2': jnp.zeros((D_MODEL,), dtype=jnp.float32)}
    _L0_ffn_in = _L0_ffn_setup()

    def _L1_attn_setup():
        import jax, jax.numpy as jnp
        import numpy as np
        B, L, D_MODEL = (4, 256, 128)
        N_HEADS, FEAT, HEAD_DIM = (16, 16, 64)
        CHUNK = 128
        EPS = 1e-12

        def taylor_exp(x):
            f = x.shape[-1]
            r2 = jnp.sqrt(jnp.asarray(2.0, x.dtype))
            rd = jnp.sqrt(jnp.asarray(float(f), x.dtype))
            rrd = jnp.sqrt(rd)
            x2 = (x[..., :, None] * x[..., None, :]).reshape(*x.shape[:-1], f * f) / r2
            ones = jnp.ones_like(x[..., :1])
            return jnp.concatenate([ones, x / rrd, x2 / rd], axis=-1)
        key = jax.random.key(seed)
        k1, k2, k3, k4, k5 = jax.random.split(key, 5)
        s = 0.02
        return {'hidden_states': jax.random.normal(k1, (B, L, D_MODEL), jnp.float32), 'Wq': jax.random.normal(k2, (N_HEADS * FEAT, D_MODEL), jnp.float32) * s, 'Wk': jax.random.normal(k3, (N_HEADS * FEAT, D_MODEL), jnp.float32) * s, 'Wv': jax.random.normal(k4, (N_HEADS * HEAD_DIM, D_MODEL), jnp.float32) * s, 'Wo': jax.random.normal(k5, (D_MODEL, N_HEADS * HEAD_DIM), jnp.float32) * s}
    _L1_attn_in = _L1_attn_setup()

    def _L1_ffn_setup():
        import jax, jax.numpy as jnp
        import numpy as np
        D_MODEL = 128
        H_SHARED = 256
        H_ROUTED = 128
        N_EXPERTS = 8
        TOP_K = 2
        key = jax.random.key(seed)
        ks = jax.random.split(key, 8)
        B, T = (2, 256)
        sc_d = 1.0 / np.sqrt(D_MODEL)
        sc_hs = 1.0 / np.sqrt(H_SHARED)
        sc_hr = 1.0 / np.sqrt(H_ROUTED)
        return {'x': jax.random.normal(ks[0], (B, T, D_MODEL), dtype=jnp.float32), 'router_w': jax.random.normal(ks[1], (N_EXPERTS, D_MODEL), dtype=jnp.float32) * sc_d, 'router_bias': jnp.zeros((N_EXPERTS,), dtype=jnp.float32), 'sw1': jax.random.normal(ks[2], (D_MODEL, H_SHARED), dtype=jnp.float32) * sc_d, 'sw3': jax.random.normal(ks[3], (D_MODEL, H_SHARED), dtype=jnp.float32) * sc_d, 'sw2': jax.random.normal(ks[4], (H_SHARED, D_MODEL), dtype=jnp.float32) * sc_hs, 'ew1': jax.random.normal(ks[5], (N_EXPERTS, D_MODEL, H_ROUTED), dtype=jnp.float32) * sc_d, 'ew2': jax.random.normal(ks[6], (N_EXPERTS, H_ROUTED, D_MODEL), dtype=jnp.float32) * sc_hr}
    _L1_ffn_in = _L1_ffn_setup()
    _d = {'L0_attn_x': _L0_attn_in['x'], 'L0_attn_Wq': _L0_attn_in['Wq'], 'L0_attn_Wk': _L0_attn_in['Wk'], 'L0_attn_Wv': _L0_attn_in['Wv'], 'L0_attn_Wo': _L0_attn_in['Wo'], 'L0_attn_gamma': _L0_attn_in['gamma'], 'L0_attn_beta': _L0_attn_in['beta'], 'L0_ffn_U1': _L0_ffn_in['U1'], 'L0_ffn_V1': _L0_ffn_in['V1'], 'L0_ffn_b1': _L0_ffn_in['b1'], 'L0_ffn_U2': _L0_ffn_in['U2'], 'L0_ffn_V2': _L0_ffn_in['V2'], 'L0_ffn_b2': _L0_ffn_in['b2'], 'L1_attn_Wq': _L1_attn_in['Wq'], 'L1_attn_Wk': _L1_attn_in['Wk'], 'L1_attn_Wv': _L1_attn_in['Wv'], 'L1_attn_Wo': _L1_attn_in['Wo'], 'L1_ffn_router_w': _L1_ffn_in['router_w'], 'L1_ffn_router_bias': _L1_ffn_in['router_bias'], 'L1_ffn_sw1': _L1_ffn_in['sw1'], 'L1_ffn_sw3': _L1_ffn_in['sw3'], 'L1_ffn_sw2': _L1_ffn_in['sw2'], 'L1_ffn_ew1': _L1_ffn_in['ew1'], 'L1_ffn_ew2': _L1_ffn_in['ew2']}
    _x0 = _d['L0_attn_x']
    _d['L0_attn_x'] = jax.random.normal(jax.random.fold_in(jax.random.key(seed), 1), (8, 512, 128), dtype=_x0.dtype)
    del _x0
    return _d

def reference(L0_attn_x, L0_attn_Wq, L0_attn_Wk, L0_attn_Wv, L0_attn_Wo, L0_attn_gamma, L0_attn_beta, L0_ffn_U1, L0_ffn_V1, L0_ffn_b1, L0_ffn_U2, L0_ffn_V2, L0_ffn_b2, L1_attn_Wq, L1_attn_Wk, L1_attn_Wv, L1_attn_Wo, L1_ffn_router_w, L1_ffn_router_bias, L1_ffn_sw1, L1_ffn_sw3, L1_ffn_sw2, L1_ffn_ew1, L1_ffn_ew2):

    def _L0_attn_ref(x, Wq, Wk, Wv, Wo, gamma, beta):
        import jax, jax.numpy as jnp
        import numpy as np
        NUM_HEADS = 16
        LN_EPS = 1e-05
        B, S, E = x.shape
        H = NUM_HEADS
        D = E // H
        scale = 1.0 / D ** 0.5
        q = x @ Wq.T
        k = x @ Wk.T * scale
        v = x @ Wv.T
        qh = q.reshape(B, S, H, D)
        kh = k.reshape(B, S, H, D)
        qk = jnp.einsum('bthd,bshd->bhts', qh, kh)
        causal = jnp.tril(jnp.ones((S, S), dtype=bool))
        qk = jnp.where(causal, qk, -jnp.inf)
        attn = jax.nn.softmax(qk, axis=-1)
        vh = v.reshape(B, S, D, H)
        qkv = jnp.einsum('bsdh,bhts->bthd', vh, attn)
        qkv = qkv.reshape(B, S, E)
        mu = jnp.mean(qkv, axis=-1, keepdims=True)
        var = jnp.mean(jnp.square(qkv - mu), axis=-1, keepdims=True)
        ln = (qkv - mu) * jax.lax.rsqrt(var + LN_EPS) * gamma + beta
        return ln @ Wo.T

    def _L0_ffn_ref(x, U1, V1, b1, U2, V2, b2):
        import jax, jax.numpy as jnp
        import numpy as np
        D_MODEL, D_FF, RANK = (128, 512, 32)
        B, S = (4, 512)
        P = jnp.einsum('bsd,dr->bsr', x, U1)
        H = jax.nn.gelu(jnp.einsum('bsr,rf->bsf', P, V1) + b1)
        Q = jnp.einsum('bsf,fr->bsr', H, U2)
        return jnp.einsum('bsr,rd->bsd', Q, V2) + b2

    def _L1_attn_ref(hidden_states, Wq, Wk, Wv, Wo):
        import jax, jax.numpy as jnp
        import numpy as np
        B, L, D_MODEL = (4, 256, 128)
        N_HEADS, FEAT, HEAD_DIM = (16, 16, 64)
        CHUNK = 128
        EPS = 1e-12

        def taylor_exp(x):
            f = x.shape[-1]
            r2 = jnp.sqrt(jnp.asarray(2.0, x.dtype))
            rd = jnp.sqrt(jnp.asarray(float(f), x.dtype))
            rrd = jnp.sqrt(rd)
            x2 = (x[..., :, None] * x[..., None, :]).reshape(*x.shape[:-1], f * f) / r2
            ones = jnp.ones_like(x[..., :1])
            return jnp.concatenate([ones, x / rrd, x2 / rd], axis=-1)
        b, l, _ = hidden_states.shape
        q = (hidden_states @ Wq.T).reshape(b, l, N_HEADS, FEAT).transpose(0, 2, 1, 3)
        k = (hidden_states @ Wk.T).reshape(b, l, N_HEADS, FEAT).transpose(0, 2, 1, 3)
        v = (hidden_states @ Wv.T).reshape(b, l, N_HEADS, HEAD_DIM).transpose(0, 2, 1, 3)
        qf = taylor_exp(q)
        kf = taylor_exp(k)
        De = qf.shape[-1]
        n = l // CHUNK
        qc = jnp.moveaxis(qf.reshape(b, N_HEADS, n, CHUNK, De), 2, 0)
        kc = jnp.moveaxis(kf.reshape(b, N_HEADS, n, CHUNK, De), 2, 0)
        vc = jnp.moveaxis(v.reshape(b, N_HEADS, n, CHUNK, HEAD_DIM), 2, 0)
        mask = jnp.tril(jnp.ones((CHUNK, CHUNK), qf.dtype))

        def step(carry, xs):
            S, z = carry
            qi, ki, vi = xs
            attn = jnp.einsum('bhid,bhjd->bhij', qi, ki) * mask
            num = jnp.einsum('bhij,bhje->bhie', attn, vi) + jnp.einsum('bhid,bhde->bhie', qi, S)
            den = attn.sum(-1) + jnp.einsum('bhid,bhd->bhi', qi, z)
            yi = num / (den[..., None] + EPS)
            S = S + jnp.einsum('bhjd,bhje->bhde', ki, vi)
            z = z + ki.sum(2)
            return ((S, z), yi)
        S0 = jnp.zeros((b, N_HEADS, De, HEAD_DIM), qf.dtype)
        z0 = jnp.zeros((b, N_HEADS, De), qf.dtype)
        _, ys = jax.lax.scan(step, (S0, z0), (qc, kc, vc))
        y = jnp.moveaxis(ys, 0, 2).reshape(b, N_HEADS, l, HEAD_DIM)
        y = y.transpose(0, 2, 1, 3).reshape(b, l, N_HEADS * HEAD_DIM)
        return y @ Wo.T

    def _L1_ffn_ref(x, router_w, router_bias, sw1, sw3, sw2, ew1, ew2):
        import jax, jax.numpy as jnp
        import numpy as np
        D_MODEL = 128
        H_SHARED = 256
        H_ROUTED = 128
        N_EXPERTS = 8
        TOP_K = 2
        B, T, C = x.shape
        xf = x.reshape(-1, C)
        shared_out = jax.nn.silu(xf @ sw1) * (xf @ sw3) @ sw2
        s = jax.nn.sigmoid((xf @ router_w.T).astype(jnp.float32))
        sel_scores = s + router_bias.astype(jnp.float32)
        _, topk_idx = jax.lax.top_k(sel_scores, TOP_K)
        s_sel = jnp.take_along_axis(s, topk_idx, axis=1)
        denom = s_sel.sum(axis=1, keepdims=True)
        gates = jnp.where(denom > 1e-09, s_sel / (denom + 1e-09), 1.0 / TOP_K).astype(x.dtype)
        one_hot = jax.nn.one_hot(topk_idx, N_EXPERTS, dtype=x.dtype)
        comb = jnp.einsum('nke,nk->ne', one_hot, gates)
        h = jax.nn.gelu(jnp.einsum('nd,edh->neh', xf, ew1), approximate=False)
        y = jnp.einsum('neh,ehd->ned', h, ew2)
        routed_out = jnp.einsum('ned,ne->nd', y, comb)
        return (shared_out + routed_out).reshape(B, T, C)
    x = L0_attn_x
    x = x + 0.5 * _L0_ffn_ref(_layernorm(x, axis=-1), L0_ffn_U1, L0_ffn_V1, L0_ffn_b1, L0_ffn_U2, L0_ffn_V2, L0_ffn_b2)
    x = x + _L0_attn_ref(_layernorm(x, axis=-1), L0_attn_Wq, L0_attn_Wk, L0_attn_Wv, L0_attn_Wo, L0_attn_gamma, L0_attn_beta)
    x = x + 0.5 * _L0_ffn_ref(_layernorm(x, axis=-1), L0_ffn_U1, L0_ffn_V1, L0_ffn_b1, L0_ffn_U2, L0_ffn_V2, L0_ffn_b2)
    x = x + 0.5 * _L1_ffn_ref(_layernorm(x, axis=-1), L1_ffn_router_w, L1_ffn_router_bias, L1_ffn_sw1, L1_ffn_sw3, L1_ffn_sw2, L1_ffn_ew1, L1_ffn_ew2)
    x = x + _L1_attn_ref(_layernorm(x, axis=-1), L1_attn_Wq, L1_attn_Wk, L1_attn_Wv, L1_attn_Wo)
    x = x + 0.5 * _L1_ffn_ref(_layernorm(x, axis=-1), L1_ffn_router_w, L1_ffn_router_bias, L1_ffn_sw1, L1_ffn_sw3, L1_ffn_sw2, L1_ffn_ew1, L1_ffn_ew2)
    return x

_drawn_inputs = setup_inputs


def setup_inputs(seed=0):
    import zlib

    import numpy as np

    out = dict(_drawn_inputs(seed))
    spreads = {'L0_attn_gamma': (1.0, 0.2),
     'L0_attn_beta': (0.0, 0.1),
     'L0_ffn_b1': (0.0, 0.341),
     'L0_ffn_b2': (0.0, 0.1),
     'L1_ffn_router_bias': (0.0, 0.1)}
    factors = {'L0_ffn_U1': 8.0,
     'L0_ffn_V1': 8.0,
     'L0_ffn_U2': 3.582,
     'L0_ffn_V2': 3.201,
     'L1_attn_Wq': 8.0,
     'L1_attn_Wk': 8.0}
    for name, (base, spread) in spreads.items():
        noise = np.random.default_rng([zlib.crc32(name.encode()), seed]).standard_normal(out[name].shape)
        drawn = base * np.exp(spread * noise) if base else spread * noise
        out[name] = jnp.asarray(drawn.astype(out[name].dtype))
    for name, factor in factors.items():
        out[name] = (out[name] * factor).astype(out[name].dtype)
    return out
```

```python
from contextlib import ExitStack

import numpy as np

import concourse.bass as bass
from concourse import mybir

F32 = mybir.dt.float32
F16 = mybir.dt.float16
BF16 = mybir.dt.bfloat16
U32 = mybir.dt.uint32
ALU = mybir.AluOpType
ACT = mybir.ActivationFunctionType
AX = mybir.AxisListType

B, S, D = 8, 512, 128
P = 128
NT = S // P
LN_EPS = 1e-5
F0, R0 = 512, 32
NF = F0 // P
H0, HD0 = 16, 8
GH = 4
NG = H0 // GH
VC = 32
OFF_ROW = 96
OFF_UNIT = 64.0
H1, FEAT, HD1 = 16, 16, 64
NPAIR = H1 // 2
TAYLOR_EPS = 1e-12
HS, HR, NE = 256, 128, 8
NS = HS // P
GATE_EPS = 1e-9
MASKED = -1e30

WIDTH = [S - P * kt for kt in range(NT)]


def segment(kt, head, heads):
    if kt == 0:
        return head * S
    if kt == 1:
        return (heads + head) * S
    if kt == 3:
        return (heads + head) * S + WIDTH[1]
    return 2 * heads * S + head * WIDTH[2]


def units_of(heads):
    return ([[(0, h)] for h in range(heads)] + [[(1, h), (3, h)] for h in range(heads)]
            + [[(2, h), (2, h + 1)] for h in range(0, heads, 2)])


UNITS0, UNITS1 = units_of(GH), units_of(2)
COLS0, COLS1 = len(UNITS0) * S, len(UNITS1) * S

ORDER_A = (["load", "norm 0", "up0 0", "down0 0", "norm 1", "qkv0", "pad0 0", "max 0", "pad0 1", "max 1",
            "shift 0", "pad0 2", "pad0 3", "max 2", "shift 1", "exp 0", "max 3", "shift 2", "exp 1", "pv0 0", "shift 3", "exp 2", "turn 0", "pv0 1",
            "exp 3", "turn 1", "pv0 2", "turn 2", "pv0 3", "turn 3", "norm 2", "out0", "norm 3", "up0 1",
            "down0 1"])
MOE = [["gates {}".format(n), "route {}".format(n)] + ["expert {}".format(NE * n + e) for e in range(NE)]
       for n in range(2)]
ORDER_B = (["take", "norm 0"] + MOE[0] + ["norm 1", "qkv1", "pad1 0", "pad1 1", "pad1 2", "pad1 3", "sq 0", "sq 1", "pv1 0"]
           + [f"{x} {p + d}" for p in range(NPAIR - 2) for x, d in (("sq", 2), ("scale", 0), ("pv1", 1))]
           + [f"scale {NPAIR - 2}", f"pv1 {NPAIR - 1}", f"scale {NPAIR - 1}", "out1", "norm 2"] + MOE[1] + ["store"])
DURATION = {"load": 2, "norm": 6, "up0": 5, "down0": 4, "qkv0": 5, "pad0": 2, "max": 8, "shift": 2, "exp": 7,
            "pv0": 3, "turn": 1, "out0": 2, "take": 1, "gates": 8, "route": 2, "expert": 3, "qkv1": 12,
            "pad1": 2, "sq": 3, "pv1": 4, "scale": 1, "out1": 8, "store": 1}


def ring_uses(step):
    name, _, n = step.partition(" ")
    n = int(n or 0)
    if name == "norm":
        return [("lnT", "act")]
    if name == "up0":
        return [(f"up{f}", "act") for f in range(NF)]
    if name in ("down0", "out0", "out1"):
        return [("y", "dve")]
    if name == "qkv0":
        return [("q", "dve"), ("k", "dve"), ("v", "act")]
    if name == "max":
        return [(f"u{u}", "dve") for u in range(len(UNITS0))]
    if name == "shift":
        return [("mT", "act")]
    if name == "exp":
        return [(f"u{u}", "act") for u in range(len(UNITS0))]
    if name == "turn":
        return [("o", "dve")]
    if name == "gates":
        return [("router", "act")] + [(f"{x}{f}", "dve") for f in range(NS) for x in ("gate", "lin")]
    if name == "expert":
        e = n % NE
        return [(f"e{k}", "act") for k in ([0, 1] if e == 0 else [e + 1] if e + 1 < NE else [])]
    if name == "qkv1":
        return ([(f"q{t}", "dve") for t in range(2)] + [(f"k{t}", "dve") for t in range(2)]
                + [(f"v{t}{c}", ("act", "dve")[c]) for t in range(NT) for c in range(2)])
    if name == "sq":
        return [(f"u{u}", "act") for u in range(len(UNITS1))]
    if name == "scale":
        return [("r", "dve")]
    return []


def unit_of_expert(n, e):
    return f"expert {NE * n + max(e - 1, 0)}", f"e{e}"


def ring_table(order, banks):
    table, drained = {}, {"act": 0, "dve": 0}
    listed = [(step, u, e) for step in order for u, e in ring_uses(step)]
    for n, (step, u, e) in enumerate(listed):
        drained[e] += 1
        before = table[listed[n - banks][:2]] if n >= banks else None
        table[step, u] = Unit(n + 1, n % banks, e, drained[e], before)
    return table, Totals(len(listed), drained["act"], drained["dve"])


def weave(a, b):
    def stamped(order, half):
        total = sum(DURATION[s.split()[0]] for s in order)
        at, out = 0.0, []
        for s in order:
            out.append((at / total, half, s))
            at += DURATION[s.split()[0]]
        return out
    return [(h, s) for _, h, s in sorted(stamped(a, "A") + stamped(b, "B"), key=lambda x: x[0])]


class Unit:

    def __init__(self, n, bank, engine, count, before):
        self.n, self.bank, self.engine, self.count, self.before = n, bank, engine, count, before


class Totals:

    def __init__(self, filled, act, dve):
        self.filled, self.act, self.dve = filled, act, dve


class Half:
    pass


def bcast(ap, n):
    return bass.AP(ap.tensor, ap.offset, [list(x) for x in ap.ap[:-1]] + [[0, n]])


class Chain:

    def __init__(self, eng, sem, per):
        self.eng, self.sem, self.per, self.n, self.it = eng, sem, per, 0, 0

    def start(self, it):
        self.it, self.n = it, 0

    def then(self, ins, apart=None):
        self.n += 1
        ins.then_inc(self.sem, 1)
        self.eng.wait_ge(self.sem, self.it * self.per + self.n)
        if apart is not None:
            apart()

    def end(self):
        assert self.n == self.per, (self.n, self.per)


def build_program(nc, x, w, cst, out):
    ctx = ExitStack()
    with ctx:
        def sb(name, shape, dt=F32):
            return ctx.enter_context(nc.sbuf_tensor(name, shape, dt))

        def sem(name):
            return ctx.enter_context(nc.semaphore(name))

        banks = [ctx.enter_context(nc.psum_tensor(f"bank{i}", [P, S], F32)) for i in range(8)]
        ringA, accA = banks[0:3], banks[3]
        ringB, numB, denB = banks[4:6], banks[6], banks[7]
        TA, PERA = ring_table(ORDER_A, len(ringA))
        TB, PERB = ring_table(ORDER_B, len(ringB))

        ident = sb("ident", [P, P])
        identb = sb("identb", [P, P], BF16)
        negmask = sb("negmask", [P, P], BF16)
        headmask = sb("headmask", [P, GH])
        pairmask = sb("pairmask", [P, 2])
        iota8 = sb("iota8", [P, NT, NE])
        ones = sb("ones", [P, 32])
        spread = sb("spread", [P, P], BF16)
        neghalf = sb("neghalf", [P, NT])
        epsilon = sb("epsilon", [P, NT])
        spare_dve = sb("spare_dve", [1, 1])
        w1 = sb("w1", [P, F0])
        w2 = sb("w2", [P, NF, D])
        b1 = sb("b1", [P, NF]); b2h = sb("b2h", [P, NT, D])
        wq0 = sb("wq0", [P, D]); wk0 = sb("wk0", [P, D]); wv0 = sb("wv0", [P, D]); wo0 = sb("wo0", [P, D])
        gb = sb("gb", [P, 2])
        wq1 = sb("wq1", [P, H1 * FEAT]); wk1 = sb("wk1", [P, H1 * FEAT]); wv1 = sb("wv1", [P, H1 * HD1])
        wo1 = sb("wo1", [P, NPAIR, D])
        rw = sb("rw", [P, NE]); rbias = sb("rbias", [P, NT, NE])
        sw1 = sb("sw1", [P, HS]); sw3 = sb("sw3", [P, HS]); sw2 = sb("sw2", [P, NS, D])
        ew1 = sb("ew1", [P, NE, HR]); ew2 = sb("ew2", [P, NE, D])

        def half(name):
            h = Half()
            h.x = sb(f"x{name}", [P, NT, D])
            h.ln = sb(f"ln{name}", [P, NT, D])
            h.lnT = sb(f"lnT{name}", [P, S])
            h.stats, h.mv = sb(f"stats{name}", [P, NT, 6]), sb(f"mv{name}", [P, NT, 2])
            h.vare, h.rstd = sb(f"vare{name}", [P, NT]), sb(f"rstd{name}", [P, NT])
            h.spare = sb(f"spare{name}", [1, 1])
            h.filled = sem(f"filled{name}")
            h.act, h.dve = sem(f"drained_act{name}"), sem(f"drained_dve{name}")
            h.x_ready = sem(f"x_ready{name}")
            h.mv_ready, h.vare_ready = sem(f"mv_ready{name}"), sem(f"vare_ready{name}")
            h.rstd_ready, h.ln_ready = sem(f"rstd_ready{name}"), sem(f"ln_ready{name}")
            h.hi_ready = sem(f"hi_ready{name}")
            h.dve_step = sem(f"dve_step{name}")
            h.carried = sem(f"carried{name}")
            return h

        A, Bh = half("A"), half("B")
        A.ring, Bh.ring, A.T, Bh.T, A.per, Bh.per = ringA, ringB, TA, TB, PERA, PERB
        A.lns, Bh.lns = 4, 3
        A.carriers, Bh.carriers = 3 * NG, NPAIR
        A.name, Bh.name = "A", "B"
        probs = sb("probs", [P, 2, COLS0])
        hid0 = probs[:, 1, 0:NF * S].rearrange("p (f s) -> p f s", f=NF)
        p16 = probs[:, 0, :].bitcast(F16)
        q0h, q0l, k0h, k0l = (p16[:, i * S:(i + 1) * S] for i in range(4))
        kall = p16[:, 4 * S:(4 + NG) * S].rearrange("p (g s) -> p g s", g=NG)
        q0a = sb("q0a", [P, NG, S], F16)
        kpad0 = sb("kpad0", [P, H0, S], F16)
        vaug = sb("vaug", [P, NT, H0, HD0 + 1])
        bmax = sb("bmax", [P, len(UNITS0) * NT])
        rmax = sb("rmax", [P, NT, H0])
        offs = sb("offs", [GH, NG, S], F16)
        oT = sb("oT", [P, 2, S])
        rden = sb("rden", [P, NT, GH, 1])
        attn = sb("attn", [P, NT, D])
        mid = sb("mid", [P, NT, D])
        yT = sb("yT", [P, NPAIR, S])
        wts = sb("wts", [P, 2, COLS1])
        sgm, hsh, hexp = yT[:, 0:NS, :], yT[:, NS:2 * NS, :], yT[:, 2 * NS:2 * NS + 2, :]
        k1a = yT[0:96, 0:NPAIR // 2, :].rearrange("p a s -> p (a s)").bitcast(F16)\
            .rearrange("p (a s) -> p a s", s=S)
        w16 = wts[:, 0, :].bitcast(F16)
        q1h, q1l, k1h, k1l = (w16[:, 2 * i * S:2 * (i + 1) * S].rearrange("p (t s) -> p t s", t=2)
                              for i in range(4))
        U1T, V1 = wts[0:R0, 0, 0:D], wts[0:R0, 0, D:D + F0]
        U2T, V2 = wts[0:R0, 1, 0:F0], wts[0:R0, 1, F0:F0 + D]
        negf = wts[:, 1, F0 + D:F0 + D + P]
        spreadf = wts[:, 1, F0 + D + P:F0 + D + 2 * P]
        s8 = sb("s8", [P, NT, NE]); sel = sb("sel", [P, NT, NE]); top = sb("top", [P, NT, 8])
        idx = sb("idx", [P, NT, 8], U32); idf = sb("idf", [P, NT, 2])
        oh = sb("oh", [P, 2, NT, NE]); pick = sb("pick", [P, NT, NE]); ssel = sb("ssel", [P, NT, NE])
        den = sb("den", [P, NT, 1]); dsafe = sb("dsafe", [P, NT, 1]); half_if = sb("half_if", [P, NT, 1])
        rdn = sb("rdn", [P, NT, 1]); rsc = sb("rsc", [P, NT, 1]); flat = sb("flat", [P, NT, 1])
        gsc = sb("gsc", [P, NT, NE]); gfl = sb("gfl", [P, NT, NE]); comb = sb("comb", [P, NT, NE])
        acc = Bh.ln
        q1a = sb("q1a", [96, NPAIR, S], F16)
        kpad1 = sb("kpad1", [96, H1, S], F16)
        v1 = sb("v1", [P, NT, H1 * HD1])
        d32 = sb("d32", [P, S])
        dlate = sb("dlate", [HD1, S // 32]); dsum = sb("dsum", [HD1, S // 32]); rrec = sb("rrec", [HD1, S // 32])
        rrem = sb("rrem", [HD1, S // 32])
        rsplit = sb("rsplit", [P, S], BF16)
        rrows = sb("rrows", [P, S], BF16)
        res = sb("res", [P, NT, D])

        w_ready = sem("w_ready"); setup = sem("setup"); negb_ready = sem("negb_ready")
        offset_rows = sem("offset_rows")
        lowrank = sem("lowrank"); lowrank_copied = sem("lowrank_copied")
        qk0_laid = [sem(f"qk0_laid{g}") for g in range(NG)]
        qk1_laid = [sem(f"qk1_laid{n}") for n in range(4)]
        kpad0_ready = sem("kpad0_ready"); kpad1_ready = sem("kpad1_ready")
        rmax_ready = sem("rmax_ready"); offs_ready = sem("offs_ready")
        offs_laid = [sem(f"offs_laid{g}") for g in range(NG)]
        masked0 = sem("masked0"); pv0_done = sem("pv0_done"); oT_ready = sem("oT_ready")
        mid_taken = sem("mid_taken")
        gate_ready = sem("gate_ready"); hsh_ready = sem("hsh_ready")
        moe_out = sem("moe_out"); moe_added = sem("moe_added")
        plus1 = sem("plus1"); masked1 = sem("masked1"); pv1_done = sem("pv1_done")
        den_done = sem("den_done"); den_read = sem("den_read"); num_read = sem("num_read")
        rrows_ready = sem("rrows_ready")
        res_free = sem("res_free")

        NW = len(w)
        DVE_A, DVE_B = 10, 85
        QK_DMAS = 6
        order_loop = weave(ORDER_A, ORDER_B)

        def steps(fns, it_of, order):
            for h, step in order:
                name, _, n = step.partition(" ")
                if name == "norm" and name in fns:
                    fns[name](A if h == "A" else Bh, it_of[h], int(n), step)
                elif name in fns:
                    fns[name](it_of[h], int(n or 0), step)

        def run(eng, fns, start=None, end=None):
            def part(it_of, order):
                if start:
                    start(it_of)
                steps(fns, it_of, order)
                if end:
                    end(it_of)
            part({"A": 0}, [("A", s) for s in ORDER_A])
            with eng.Fori(0, B - 1) as i:
                part({"A": i + 1, "B": i}, order_loop)
            part({"B": B - 1}, [("B", s) for s in ORDER_B])

        def fill(pe, h, it, step, unit):
            u = h.T[step, unit]
            if u.before:
                s = {"act": h.act, "dve": h.dve}[u.before.engine]
                pe.wait_ge(s, it * (h.per.act if u.before.engine == "act" else h.per.dve) + u.before.count)
            return h.ring[u.bank]

        def full(eng, h, it, step, unit):
            u = h.T[step, unit]
            eng.wait_ge(h.filled, it * h.per.filled + u.n)
            return h.ring[u.bank]

        def drained(h, it, step, unit):
            u = h.T[step, unit]
            return it * (h.per.act if u.engine == "act" else h.per.dve) + u.count

        block = ctx.enter_context(nc.Block())

        @block.sync
        def _(sp):
            for dst, src in ((ident[:], cst["ident"]), (negf, cst["negmask"]), (spreadf, cst["spread"]), (headmask[:], cst["headmask"]),
                             (pairmask[:], cst["pairmask"]), (iota8[:], cst["iota8"])):
                sp.dma_start(dst, src).then_inc(w_ready, 16)
            tiles = dict(U1T=U1T, V1=V1, U2T=U2T, V2=V2, b1=b1[:], b2=b2h[:], wq0=wq0[:], wk0=wk0[:], wv0=wv0[:], wo0=wo0[:],
                         gb=gb[:], wq1=wq1[:], wk1=wk1[:], wv1=wv1[:], wo1=wo1[:], rw=rw[:], rbias=rbias[:], sw1=sw1[:], sw3=sw3[:],
                         sw2=sw2[:], ew1=ew1[:], ew2=ew2[:])
            for name, src in w.items():
                sp.dma_start(tiles[name], src).then_inc(w_ready, 16)

            def load(it, _n, step):
                if not isinstance(it, int):
                    sp.wait_ge(A.dve, drained(A, it, "down0 1", "y") - A.per.dve)
                sp.dma_start(A.x[:, :, :], x[bass.ds(it, 1), :, :].rearrange("a (t p) d -> p (a t) d", p=P))\
                  .then_inc(A.x_ready, 16)

            def qkv0(it, _n, step):
                sp.wait_ge(A.dve, drained(A, it, step, "k"))
                for g in range(NG):
                    rows = slice(32 * g, 32 * g + 32)
                    for dst, parts in ((q0a, (q0h, q0h, q0l)), (kall, (k0h, k0l, k0h))):
                        for a, part in enumerate(parts):
                            sp.dma_start(dst[32 * a:32 * a + 32, g, :], part[rows, :]).then_inc(qk0_laid[g], 16)

            def shift(it, g, step):
                sp.wait_ge(A.act, drained(A, it, step, "mT"))
                sp.dma_start(q0a[OFF_ROW:OFF_ROW + GH, g, :], offs[:, g, :]).then_inc(offs_laid[g], 16)

            def qkv1(it, _n, step):
                sp.wait_ge(Bh.dve, drained(Bh, it, step, "k1"))
                for n in range(4):
                    rows = slice(32 * n, 32 * n + 32)
                    for dst, parts in ((q1a, (q1h, q1h, q1l)), (k1a, (k1h, k1l, k1h))):
                        for a, part in enumerate(parts):
                            sp.dma_start(dst[32 * a:32 * a + 32, n:NPAIR:4, :], part[rows, :, :])\
                              .then_inc(qk1_laid[n], 16)

            def store(it, _n, step):
                sp.wait_ge(moe_added, (it * 2 + 2) * (NE + 1))
                sp.dma_start(out[bass.ds(it, 1), :, :].rearrange("a (t p) d -> p (a t) d", p=P), res[:, :, :])\
                  .then_inc(res_free, 16)

            run(sp, dict(load=load, qkv0=qkv0, shift=shift, qkv1=qkv1, store=store))
            sp.wait_ge(res_free, 16 * (B + 1))

        @block.gpsimd
        def _(pool):
            pool.memset(vaug[:, :, :, HD0:HD0 + 1], 1.0).then_inc(setup, 1)
            pool.memset(neghalf[:, :], -0.5).then_inc(setup, 1)
            pool.memset(epsilon[:, :], LN_EPS).then_inc(setup, 1)
            pool.memset(ones[:, :], 1.0).then_inc(setup, 1)
            pool.wait_ge(setup, 9)
            for h in (A, Bh):
                pool.tensor_tensor(h.spare[:, :], neghalf[0:1, 0:1], neghalf[0:1, 0:1], ALU.add).then_inc(h.carried, 1)

            def ln_scale(h, it, k, step):
                pool.wait_ge(h.mv_ready, it * h.lns + k + 1)
                pool.tensor_tensor(h.vare[:, :], h.mv[:, :, 1], epsilon[:, :], ALU.add).then_inc(h.vare_ready, 1)
                pool.wait_ge(h.vare_ready, it * h.lns + k + 1)
                pool.tensor_tensor(h.rstd[:, :], h.vare[:, :], neghalf[:, :], ALU.pow).then_inc(h.rstd_ready, 1)

            def wait_apart(h, it, n, sem, value):
                pool.wait_ge(h.carried, it * h.carriers + n + 1)
                pool.wait_ge(sem, value)
                pool.tensor_tensor(h.spare[:, :], neghalf[0:1, 0:1], neghalf[0:1, 0:1], ALU.add).then_inc(h.carried, 1)

            def mask(buf, heads, kt):
                step = {0: S, 1: S, 3: S, 2: WIDTH[2]}[kt]
                s0 = segment(kt, 0, heads)
                v = bass.AP(buf.tensor, buf.offset + s0, [list(buf.ap[0]), [step, heads], [1, P]])
                return pool.affine_select(out=v, in_=v, compare_op=ALU.is_ge, fill=0.0, base=0,
                                          pattern=[[0, heads], [1, P]], channel_multiplier=-1)

            def exp(it, g, step):
                for kt, last in ((0, GH - 1), (1, 2 * GH - 1), (3, None), (2, len(UNITS0) - 1)):
                    if last is not None:
                        wait_apart(A, it, g * 3 + (0, 1, 2, 1)[kt], A.act, drained(A, it, step, f"u{last}"))
                    mask(probs[:, g % 2, :], GH, kt).then_inc(masked0, 1)

            def sq(it, p, step):
                wait_apart(Bh, it, p, plus1, it * NPAIR + p + 1)
                for kt in (0, 1, 3, 2):
                    mask(wts[:, p % 2, :], 2, kt).then_inc(masked1, 1)

            run(pool, dict(norm=ln_scale, exp=exp, sq=sq))

        @block.scalar
        def _(act):
            act.wait_ge(w_ready, 16 * (NW + 6))
            act.activation(identb[:, :], ident[:, :], ACT.Copy).then_inc(negb_ready, 1)
            act.activation(negmask[:, :], negf[:, :], ACT.Copy).then_inc(negb_ready, 1)
            act.activation(spread[:, :], spreadf[:, :], ACT.Copy).then_inc(negb_ready, 1)
            act.wait_ge(lowrank, 1)
            act.activation(w1[:, :], ringA[0][:, :], ACT.Copy).then_inc(lowrank_copied, 1)
            act.activation(w2[:, :, :].rearrange("p a b -> p (a b)"), ringA[1][:, :], ACT.Copy)\
               .then_inc(lowrank_copied, 1)

            def norm(h, it, k, step):
                ps = full(act, h, it, step, "lnT")
                if h is A and k == 2:
                    act.activation(h.lnT[:, :], ps[:, :], ACT.Identity, bias=gb[:, 1:2], scale=gb[:, 0:1])\
                       .then_inc(h.act, 1)
                else:
                    act.activation(h.lnT[:, :], ps[:, :], ACT.Copy).then_inc(h.act, 1)

            def up0(it, n, step):
                for f in range(NF):
                    ps = full(act, A, it, step, f"up{f}")
                    act.activation(hid0[:, f, :], ps[:, :], ACT.Gelu_apprx_tanh, bias=b1[:, f:f + 1])\
                       .then_inc(A.act, 1)

            def qkv0(it, n, step):
                ps = full(act, A, it, step, "q")
                act.activation(q0h[:, :], ps[:, :], ACT.Copy).then_inc(A.hi_ready, 1)
                ps = full(act, A, it, step, "k")
                act.activation(k0h[:, :], ps[:, :], ACT.Copy, scale=HD0 ** -0.5).then_inc(A.hi_ready, 1)
                ps = full(act, A, it, step, "v")
                act.wait_ge(setup, 9)
                act.activation(vaug[:, :, :, 0:HD0].rearrange("p t h d -> p (t h) d"),
                               ps[:, :].rearrange("p (a d) -> p a d", d=HD0), ACT.Copy).then_inc(A.act, 1)

            def shift(it, g, step):
                ps = full(act, A, it, step, "mT")
                act.activation(offs[:, g, :], ps[0:GH, :], ACT.Copy, scale=-1.0 / OFF_UNIT).then_inc(A.act, 1)

            def exp(it, g, step):
                if g == 0:
                    act.wait_ge(kpad0_ready, it * NG + NG)
                if g >= 2:
                    act.wait_ge(pv0_done, it * NG + g - 1)
                for u in range(len(UNITS0)):
                    ps = full(act, A, it, step, f"u{u}")
                    act.activation(probs[:, g % 2, u * S:(u + 1) * S], ps[:, :], ACT.Exp).then_inc(A.act, 1)

            def gates(it, n, step):
                ps = full(act, Bh, it, step, "router")
                act.activation(s8[:, :, :].rearrange("p t e -> p (t e)"), ps[:, 0:NT * NE], ACT.Sigmoid)\
                   .then_inc(Bh.act, 1)
                for f in range(NS):
                    ps = full(act, Bh, it, step, f"gate{f}")
                    act.activation(sgm[:, f, :], ps[:, :], ACT.Sigmoid).then_inc(gate_ready, 1)

            def expert(it, n, step):
                for unit, _ in ring_uses(step):
                    e = int(unit[1:])
                    ps = full(act, Bh, it, step, unit)
                    if e >= 2:
                        act.wait_ge(moe_out, (it * 2 + n // NE) * (NE + 1) + 1 + e - 1)
                    act.activation(hexp[:, e % 2, :], ps[:, :], ACT.Gelu).then_inc(Bh.act, 1)

            def qkv1(it, n, step):
                for name, hi in (("q", q1h), ("k", k1h)):
                    for t in range(2):
                        ps = full(act, Bh, it, step, f"{name}{t}")
                        act.activation(hi[:, t, :], ps[:, :], ACT.Copy).then_inc(Bh.hi_ready, 1)
                for t in range(NT):
                    ps = full(act, Bh, it, step, f"v{t}0")
                    act.activation(v1[:, t, 0:S], ps[:, :], ACT.Copy).then_inc(Bh.act, 1)

            def sq(it, p, step):
                if p == 0:
                    act.wait_ge(kpad1_ready, it * 4 + 4)
                if p >= 2:
                    act.wait_ge(pv1_done, it * NPAIR + p - 1)
                for u in range(len(UNITS1)):
                    ps = full(act, Bh, it, step, f"u{u}")
                    act.activation(wts[:, p % 2, u * S:(u + 1) * S], ps[:, :], ACT.Square,
                                   bias=1.0, scale=FEAT ** -0.5).then_inc(Bh.act, 1)

            def pv1(it, p, step):
                act.wait_ge(pv1_done, it * NPAIR + p + 1)
                act.activation(yT[:, p, :], numB[:, :], ACT.Copy).then_inc(num_read, 1)

            run(act, dict(norm=norm, up0=up0, qkv0=qkv0, shift=shift, exp=exp, gates=gates, expert=expert,
                          qkv1=qkv1, sq=sq, pv1=pv1))

        @block.vector
        def _(dve):
            def carrier():
                dve.memset(spare_dve[:, :], 0.0)

            chA, chB = Chain(dve, A.dve_step, DVE_A), Chain(dve, Bh.dve_step, DVE_B)
            dve.wait_ge(w_ready, 16 * (NW + 6))
            dve.tensor_scalar(b2h[:, :, :], b2h[:, :, :], 0.5, None, ALU.mult).then_inc(setup, 1)
            dve.memset(accA[:, :], 0.0).then_inc(setup, 1)
            dve.memset(rsplit[:, :], 0.0).then_inc(setup, 1)
            dve.memset(dlate[:, :], 0.0).then_inc(setup, 1)
            dve.memset(q0a[OFF_ROW:P, :, :], 0.0).then_inc(setup, 1)
            dve.memset(kpad0[OFF_ROW:P, :, :], OFF_UNIT).then_inc(offset_rows, 1)
            dve.wait_ge(offset_rows, 1)
            for hd in range(H0):
                dve.tensor_scalar(kpad0[OFF_ROW:P, hd, :], kpad0[OFF_ROW:P, hd, :],
                                  headmask[OFF_ROW:P, hd % GH:hd % GH + 1], None, ALU.mult)
            dve.memset(res[:, :, :], 0.0).then_inc(res_free, 16)
            dve.wait_ge(setup, 9)

            def norm(h, it, k, step):
                ch, src = (chA, attn if k == 2 else A.x) if h is A else (chB, Bh.x)
                if h is A and k == 0:
                    dve.wait_ge(A.x_ready, (it + 1) * 16)
                elif h is A:
                    before = {1: ("down0 0", "y"), 2: (f"turn {NG - 1}", "o"), 3: ("out0", "y")}[k]
                    dve.wait_ge(A.dve, drained(A, it, *before))
                elif k == 0:
                    dve.wait_ge(mid_taken, it + 1)
                elif k == 1:
                    dve.wait_ge(moe_added, (it * 2 + 1) * (NE + 1))
                else:
                    dve.wait_ge(Bh.dve, drained(Bh, it, "out1", "y"))
                for t in range(NT):
                    last = dve.bn_stats(h.stats[:, t, :], src[:, t, :])
                ch.then(last, carrier)
                for t in range(NT):
                    last = dve.bn_aggr(h.mv[:, t, :], h.stats[:, t, :])
                last.then_inc(h.mv_ready, 1)
                dve.wait_ge(h.rstd_ready, it * h.lns + k + 1)
                for t in range(NT):
                    last = dve.tensor_scalar(h.ln[:, t, :], src[:, t, :], h.mv[:, t, 0:1], h.rstd[:, t:t + 1],
                                             ALU.subtract, ALU.mult)
                last.then_inc(h.ln_ready, 1)

            def down0(it, n, step):
                full(dve, A, it, f"norm {(0, 3)[n]}", "lnT")
                chA.then(dve.tensor_tensor(A.ln[:, :, :], A.x[:, :, :], b2h[:, :, :], ALU.add))
                ps = full(dve, A, it, step, "y")
                dst = A.x if n == 0 else mid
                if n == 1 and not isinstance(it, int):
                    dve.wait_ge(mid_taken, it)
                dve.scalar_tensor_tensor(out=dst[:, :, :].rearrange("p t d -> p (t d)"), in0=ps[:, :],
                                         scalar=0.5, in1=A.ln[:, :, :].rearrange("p t d -> p (t d)"),
                                         op0=ALU.mult, op1=ALU.add).then_inc(A.dve, 1)

            def qkv0(it, n, step):
                for i, (name, hi, lo, sc) in enumerate((("q", q0h, q0l, 1.0), ("k", k0h, k0l, HD0 ** -0.5))):
                    ps = full(dve, A, it, step, name)
                    dve.wait_ge(A.hi_ready, it * 2 + i + 1)
                    dve.scalar_tensor_tensor(out=lo[:, :], in0=ps[:, :], scalar=sc, in1=hi[:, :],
                                             op0=ALU.mult, op1=ALU.subtract).then_inc(A.dve, 1)

            def pad0(it, g, step):
                dve.wait_ge(qk0_laid[g], (it + 1) * 16 * QK_DMAS)
                dve.memset(q0a[OFF_ROW:P, g, :], 0.0)
                for hd in range(GH * g, GH * g + GH):
                    last = dve.tensor_scalar(kpad0[0:OFF_ROW, hd, :], kall[0:OFF_ROW, g, :],
                                             headmask[0:OFF_ROW, hd % GH:hd % GH + 1], None, ALU.mult)
                last.then_inc(kpad0_ready, 1)

            def rowmax(it, g, step):
                for u in range(len(UNITS0)):
                    ps = full(dve, A, it, step, f"u{u}")
                    dve.tensor_reduce(bmax[:, u * NT:(u + 1) * NT], ps[:, :].rearrange("p (b k) -> p b k", k=P),
                                      AX.X, ALU.max).then_inc(A.dve, 1)
                dve.wait_ge(A.dve, drained(A, it, step, f"u{len(UNITS0) - 1}"))
                heads = slice(g * GH, (g + 1) * GH)
                wide = bmax[:, 0:GH * NT].rearrange("p (h b) -> p h b", b=NT)
                pair = bmax[:, GH * NT:2 * GH * NT].rearrange("p (h b) -> p h b", b=NT)
                two = bmax[:, 2 * GH * NT:].rearrange("p (h b) -> p h b", b=2)
                dve.tensor_reduce(rmax[:, 3, heads], wide, AX.X, ALU.max)
                dve.tensor_reduce(rmax[:, 2, heads], pair[:, :, 0:3], AX.X, ALU.max)
                dve.tensor_reduce(rmax[:, 1, heads], two, AX.X, ALU.max)
                dve.tensor_reduce(rmax[:, 0, heads], pair[:, :, 3:4], AX.X, ALU.max).then_inc(rmax_ready, 1)
                dve.wait_ge(rmax_ready, it * NG + g + 1)

            def pv0(it, g, step):
                dve.wait_ge(pv0_done, it * NG + g + 1)
                dve.tensor_copy(oT[:, g % 2, :], accA[:, :]).then_inc(oT_ready, 1)

            def turn(it, g, step):
                ps = full(dve, A, it, step, "o")
                v = ps[:, :].rearrange("p (t h c) -> p t h c", t=NT, c=VC)
                chA.then(dve.reciprocal(rden[:, :, :, :], v[:, :, :, HD0:HD0 + 1]))
                dst = attn[:, :, g * GH * HD0:(g + 1) * GH * HD0].rearrange("p t (h c) -> p t h c", c=HD0)
                dve.tensor_tensor(dst, v[:, :, :, 0:HD0], bcast(rden[:, :, :, :], HD0), ALU.mult)\
                   .then_inc(A.dve, 1)

            def out0(it, n, step):
                ps = full(dve, A, it, step, "y")
                dve.tensor_tensor(A.x[:, :, :].rearrange("p t d -> p (t d)"), ps[:, :],
                                  A.x[:, :, :].rearrange("p t d -> p (t d)"), ALU.add).then_inc(A.dve, 1)

            def take(it, n, step):
                dve.wait_ge(A.dve, drained(A, it, "down0 1", "y"))
                dve.tensor_copy(Bh.x[:, :, :], mid[:, :, :]).then_inc(mid_taken, 1)

            def route(it, n, step):
                c = chB
                dve.wait_ge(Bh.act, drained(Bh, it, f"gates {n}", "router"))
                c.then(dve.tensor_tensor(sel[:, :, :], s8[:, :, :], rbias[:, :, :], ALU.add), carrier)
                for t in range(NT):
                    last = dve.max(top[:, t, :], sel[:, t, :])
                c.then(last, carrier)
                for t in range(NT):
                    last = dve.max_index(idx[:, t, :], top[:, t, :], sel[:, t, :])
                c.then(last)
                c.then(dve.tensor_copy(idf[:, :, :], idx[:, :, 0:2]))
                for j in range(2):
                    last = dve.tensor_tensor(oh[:, j, :, :], iota8[:, :, :], bcast(idf[:, :, j:j + 1], NE),
                                             ALU.is_equal)
                c.then(last)
                c.then(dve.tensor_tensor(pick[:, :, :], oh[:, 0, :, :], oh[:, 1, :, :], ALU.add))
                c.then(dve.tensor_tensor(ssel[:, :, :], s8[:, :, :], pick[:, :, :], ALU.mult))
                c.then(dve.tensor_reduce(den[:, :, :], ssel[:, :, :], AX.X, ALU.add))
                dve.tensor_scalar(dsafe[:, :, :], den[:, :, :], GATE_EPS, None, ALU.add)
                c.then(dve.tensor_scalar(half_if[:, :, :], den[:, :, :], GATE_EPS, 0.5, ALU.is_gt, ALU.mult))
                c.then(dve.reciprocal(rdn[:, :, :], dsafe[:, :, :]))
                dve.tensor_scalar(flat[:, :, :], half_if[:, :, :], -0.5, 0.25, ALU.mult, ALU.add)
                c.then(dve.tensor_tensor(rsc[:, :, :], rdn[:, :, :], half_if[:, :, :], ALU.mult))
                dve.tensor_tensor(gsc[:, :, :], ssel[:, :, :], bcast(rsc[:, :, :], NE), ALU.mult)
                c.then(dve.tensor_tensor(gfl[:, :, :], pick[:, :, :], bcast(flat[:, :, :], NE), ALU.mult))
                c.then(dve.tensor_tensor(comb[:, :, :], gsc[:, :, :], gfl[:, :, :], ALU.add))

            def gates(it, n, step):
                k = it * 2 + n
                for f in range(NS):
                    ps = full(dve, Bh, it, step, f"gate{f}")
                    dve.wait_ge(gate_ready, k * NS + f + 1)
                    dve.tensor_tensor(sgm[:, f, :], ps[:, :], sgm[:, f, :], ALU.mult).then_inc(Bh.dve, 1)
                    dve.wait_ge(Bh.dve, drained(Bh, it, step, f"gate{f}"))
                    ps = full(dve, Bh, it, step, f"lin{f}")
                    dve.tensor_tensor(hsh[:, f, :], ps[:, :], sgm[:, f, :], ALU.mult).then_inc(Bh.dve, 1)

            def expert(it, ne, step):
                n, e = ne // NE, ne % NE
                first = (it * 2 + n) * (NE + 1)
                if e == 0:
                    dve.wait_ge(moe_out, first + 1)
                    dve.scalar_tensor_tensor(out=acc[:, :, :].rearrange("p t d -> p (t d)"), in0=numB[:, :],
                                             scalar=0.5, in1=Bh.x[:, :, :].rearrange("p t d -> p (t d)"),
                                             op0=ALU.mult, op1=ALU.add).then_inc(moe_added, 1)
                dve.wait_ge(moe_out, first + 2 + e)
                dve.wait_ge(moe_added, first + 1 + e)
                ps, dst = (denB, numB)[e % 2], acc
                if e == NE - 1:
                    dst = (Bh.x, res)[n]
                    if n == 1:
                        dve.wait_ge(res_free, 16 * (it + 1))
                for t in range(NT):
                    last = dve.scalar_tensor_tensor(out=dst[:, t, :], in0=ps[:, t * P:(t + 1) * P],
                                                    scalar=comb[:, t, e:e + 1], in1=acc[:, t, :],
                                                    op0=ALU.mult, op1=ALU.add)
                last.then_inc(moe_added, 1)

            def qkv1(it, n, step):
                for i, (name, t, hi, lo) in enumerate((("q", 0, q1h, q1l), ("q", 1, q1h, q1l),
                                                       ("k", 0, k1h, k1l), ("k", 1, k1h, k1l))):
                    ps = full(dve, Bh, it, step, f"{name}{t}")
                    dve.wait_ge(Bh.hi_ready, it * 4 + i + 1)
                    dve.tensor_tensor(lo[:, t, :], ps[:, :], hi[:, t, :], ALU.subtract).then_inc(Bh.dve, 1)
                for t in range(NT):
                    ps = full(dve, Bh, it, step, f"v{t}1")
                    dve.tensor_copy(v1[:, t, S:2 * S], ps[:, :]).then_inc(Bh.dve, 1)

            def pad1(it, n, step):
                dve.wait_ge(qk1_laid[n], (it + 1) * 16 * QK_DMAS)
                for hd in (2 * n, 2 * n + 1, 2 * n + 8, 2 * n + 9):
                    last = dve.tensor_scalar(kpad1[:, hd, :], k1a[:, hd // 2, :], pairmask[0:96, hd % 2:hd % 2 + 1],
                                             None, ALU.mult)
                last.then_inc(kpad1_ready, 1)

            def sq(it, p, step):
                dve.wait_ge(Bh.act, drained(Bh, it, step, f"u{len(UNITS1) - 1}"))
                dve.tensor_scalar(wts[:, p % 2, :], wts[:, p % 2, :], 1.0, None, ALU.add).then_inc(plus1, 1)

            def pv1(it, p, step):
                dve.wait_ge(den_done, it * NPAIR + p + 1)
                dve.transpose(d32[:, :], denB[:, :]).then_inc(den_read, 1)
                dve.wait_ge(den_read, it * NPAIR + p + 1)
                v = d32[:, :].rearrange("p (b c) -> p b c", c=32)
                part = rsplit[0:HD1, :].rearrange("p (b c) -> p b c", c=32)
                nb = P // 32
                chB.then(dve.tensor_copy(dlate[:, nb:], v[HD1:P, nb:, 0]))
                chB.then(dve.scalar_tensor_tensor(out=dsum[:, :], in0=v[0:HD1, :, 0], scalar=2 * TAYLOR_EPS,
                                                  in1=dlate[:, :], op0=ALU.add, op1=ALU.add))
                chB.then(dve.reciprocal(rrec[:, :], dsum[:, :]))
                chB.then(dve.tensor_copy(part[:, :, 0], rrec[:, :]))
                chB.then(dve.tensor_tensor(rrem[:, :], rrec[:, :], part[:, :, 0], ALU.subtract))
                chB.then(dve.tensor_copy(part[:, :, 1], rrem[:, :]))
                chB.then(dve.tensor_tensor(part[:, :, 2], rrem[:, :], part[:, :, 1], ALU.subtract))
                dve.transpose(rrows[:, :], rsplit[:, :]).then_inc(rrows_ready, 1)

            def scale(it, p, step):
                ps = full(dve, Bh, it, step, "r")
                dve.wait_ge(num_read, it * NPAIR + p + 1)
                dve.tensor_tensor(yT[:, p, :], ps[:, :], yT[:, p, :], ALU.mult).then_inc(Bh.dve, 1)

            def out1(it, n, step):
                ps = full(dve, Bh, it, step, "y")
                dve.tensor_tensor(Bh.x[:, :, :].rearrange("p t d -> p (t d)"), ps[:, :],
                                  Bh.x[:, :, :].rearrange("p t d -> p (t d)"), ALU.add).then_inc(Bh.dve, 1)

            def start(it_of):
                for h, ch in (("A", chA), ("B", chB)):
                    if h in it_of:
                        ch.start(it_of[h])

            def end(it_of):
                for h, ch in (("A", chA), ("B", chB)):
                    if h in it_of:
                        ch.end()

            fns = dict(norm=norm, down0=down0, qkv0=qkv0, pad0=pad0, pv0=pv0, turn=turn, out0=out0, take=take,
                       gates=gates, route=route, expert=expert, qkv1=qkv1, pad1=pad1, sq=sq, pv1=pv1,
                       scale=scale, out1=out1)
            fns["max"] = rowmax
            run(dve, fns, start, end)

        @block.tensor
        def _(pe):
            mm = nc.tensor.matmul
            pe.wait_ge(w_ready, 16 * (NW + 6))
            mm(ringA[0][:, :], U1T[:, :], V1[:, :], start=True, stop=True)
            for f in range(NF):
                last = mm(ringA[1][:, f * D:(f + 1) * D], U2T[:, f * P:(f + 1) * P], V2[:, :], start=True, stop=True)
            last.then_inc(lowrank, 1)
            pe.wait_ge(lowrank_copied, 2)
            pe.wait_ge(negb_ready, 3)
            pe.wait_ge(setup, 9)

            def norm(h, it, k, step):
                pe.wait_ge(h.ln_ready, it * h.lns + k + 1)
                ps = fill(pe, h, it, step, "lnT")
                for t in range(NT):
                    last = nc.tensor.transpose(ps[:, t * P:(t + 1) * P], h.ln[:, t, :], ident[:, :])
                last.then_inc(h.filled, 1)

            def up0(it, n, step):
                pe.wait_ge(A.act, drained(A, it, f"norm {(0, 3)[n]}", "lnT"))
                for f in range(NF):
                    ps = fill(pe, A, it, step, f"up{f}")
                    mm(ps[:, :], w1[:, f * P:(f + 1) * P], A.lnT[:, :], start=True, stop=True).then_inc(A.filled, 1)

            def down0(it, n, step):
                ps = fill(pe, A, it, step, "y")
                pe.wait_ge(A.act, drained(A, it, f"up0 {n}", f"up{NF - 1}"))
                for t in range(NT):
                    for f in range(NF):
                        last = mm(ps[:, t * P:(t + 1) * P], hid0[:, f, t * P:(t + 1) * P], w2[:, f, :],
                                  start=f == 0, stop=f == NF - 1)
                last.then_inc(A.filled, 1)

            def qkv0(it, n, step):
                pe.wait_ge(A.act, drained(A, it, "norm 1", "lnT"))
                for name, wt in (("q", wq0), ("k", wk0)):
                    ps = fill(pe, A, it, step, name)
                    mm(ps[:, :], wt[:, :], A.lnT[:, :], start=True, stop=True).then_inc(A.filled, 1)
                ps = fill(pe, A, it, step, "v")
                for t in range(NT):
                    last = mm(ps[:, t * P:(t + 1) * P], A.lnT[:, t * P:(t + 1) * P], wv0[:, :], start=True, stop=True)
                last.then_inc(A.filled, 1)

            def rowmax(it, g, step):
                pe.wait_ge(kpad0_ready, it * NG + g + 1)
                for u, parts in enumerate(UNITS0):
                    ps = fill(pe, A, it, step, f"u{u}")
                    for kt, j in parts:
                        qt, c0 = NT - 1 - kt, segment(kt, j, GH) - u * S
                        n_keys = (qt + 1) * P
                        mm(ps[:, c0:c0 + n_keys], q0a[:, g, qt * P:(qt + 1) * P],
                           kpad0[:, g * GH + j, 0:n_keys], start=True, stop=False)
                        last = mm(ps[:, c0 + n_keys - P:c0 + n_keys], identb[:, :], negmask[:, :],
                                  start=False, stop=True)
                    last.then_inc(A.filled, 1)

            def shift(it, g, step):
                pe.wait_ge(rmax_ready, it * NG + g + 1)
                ps = fill(pe, A, it, step, "mT")
                for t in range(NT):
                    last = nc.tensor.transpose(ps[0:GH, t * P:(t + 1) * P], rmax[:, t, g * GH:(g + 1) * GH],
                                               ident[:, :])
                last.then_inc(A.filled, 1)

            def exp(it, g, step):
                pe.wait_ge(offs_laid[g], (it + 1) * 16)
                for u, parts in enumerate(UNITS0):
                    ps = fill(pe, A, it, step, f"u{u}")
                    for kt, j in parts:
                        c0 = segment(kt, j, GH) - u * S
                        last = mm(ps[:, c0:c0 + WIDTH[kt]], kpad0[:, g * GH + j, kt * P:(kt + 1) * P],
                                  q0a[:, g, kt * P:S], start=True, stop=True)
                    last.then_inc(A.filled, 1)

            def pv0(it, g, step):
                if g:
                    pe.wait_ge(oT_ready, it * NG + g)
                for i, kt in enumerate((0, 1, 3, 2)):
                    pe.wait_ge(masked0, it * NG * NT + g * NT + i + 1)
                    for j in range(GH):
                        c0 = segment(kt, j, GH)
                        last = mm(accA[VC * j:VC * j + HD0 + 1, kt * P:S], vaug[:, kt, g * GH + j, :],
                                  probs[:, g % 2, c0:c0 + WIDTH[kt]], start=kt == 0, stop=kt == 2)
                last.then_inc(pv0_done, 1)

            def turn(it, g, step):
                pe.wait_ge(oT_ready, it * NG + g + 1)
                ps = fill(pe, A, it, step, "o")
                for t in range(NT):
                    last = nc.tensor.transpose(ps[:, t * P:(t + 1) * P], oT[:, g % 2, t * P:(t + 1) * P], ident[:, :])
                last.then_inc(A.filled, 1)

            def out0(it, n, step):
                pe.wait_ge(A.act, drained(A, it, "norm 2", "lnT"))
                ps = fill(pe, A, it, step, "y")
                for t in range(NT):
                    last = mm(ps[:, t * P:(t + 1) * P], A.lnT[:, t * P:(t + 1) * P], wo0[:, :], start=True, stop=True)
                last.then_inc(A.filled, 1)

            def gates(it, n, step):
                pe.wait_ge(Bh.act, drained(Bh, it, f"norm {(0, 2)[n]}", "lnT"))
                ps = fill(pe, Bh, it, step, "router")
                for t in range(NT):
                    last = mm(ps[:, t * NE:(t + 1) * NE], Bh.lnT[:, t * P:(t + 1) * P], rw[:, :], start=True, stop=True)
                last.then_inc(Bh.filled, 1)
                for f in range(NS):
                    for name, wt in (("gate", sw1), ("lin", sw3)):
                        ps = fill(pe, Bh, it, step, f"{name}{f}")
                        mm(ps[:, :], wt[:, f * P:(f + 1) * P], Bh.lnT[:, :], start=True, stop=True)\
                            .then_inc(Bh.filled, 1)

            def expert(it, ne, step):
                n, e = ne // NE, ne % NE
                first = (it * 2 + n) * (NE + 1)
                for unit, _ in ring_uses(step):
                    ps = fill(pe, Bh, it, step, unit)
                    mm(ps[:, :], ew1[:, int(unit[1:]), :], Bh.lnT[:, :], start=True, stop=True).then_inc(Bh.filled, 1)
                if e == 0:
                    pe.wait_ge(Bh.dve, drained(Bh, it, f"gates {n}", f"lin{NS - 1}"))
                    for t in range(NT):
                        for f in range(NS):
                            last = mm(numB[:, t * P:(t + 1) * P], hsh[:, f, t * P:(t + 1) * P], sw2[:, f, :],
                                      start=f == 0, stop=f == NS - 1)
                    last.then_inc(moe_out, 1)
                else:
                    pe.wait_ge(moe_added, first + e)
                pe.wait_ge(Bh.act, drained(Bh, it, *unit_of_expert(n, e)))
                ps = (denB, numB)[e % 2]
                for t in range(NT):
                    last = mm(ps[:, t * P:(t + 1) * P], hexp[:, e % 2, t * P:(t + 1) * P], ew2[:, e, :],
                              start=True, stop=True)
                last.then_inc(moe_out, 1)

            def qkv1(it, n, step):
                pe.wait_ge(Bh.act, drained(Bh, it, "norm 1", "lnT"))
                for name, wt in (("q", wq1), ("k", wk1)):
                    for t in range(2):
                        ps = fill(pe, Bh, it, step, f"{name}{t}")
                        mm(ps[:, :], wt[:, t * P:(t + 1) * P], Bh.lnT[:, :], start=True, stop=True)\
                            .then_inc(Bh.filled, 1)
                for t in range(NT):
                    for c in range(2):
                        ps = fill(pe, Bh, it, step, f"v{t}{c}")
                        mm(ps[:, :], Bh.lnT[:, t * P:(t + 1) * P], wv1[:, c * S:(c + 1) * S], start=True, stop=True)\
                            .then_inc(Bh.filled, 1)

            def sq(it, p, step):
                if p < 4:
                    pe.wait_ge(kpad1_ready, it * 4 + p + 1)
                for u, parts in enumerate(UNITS1):
                    ps = fill(pe, Bh, it, step, f"u{u}")
                    for kt, j in parts:
                        c0 = segment(kt, j, 2) - u * S
                        last = mm(ps[:, c0:c0 + WIDTH[kt]], kpad1[:, 2 * p + j, kt * P:(kt + 1) * P],
                                  q1a[:, p, kt * P:S], start=True, stop=True)
                    last.then_inc(Bh.filled, 1)

            def pv1(it, p, step):
                if p:
                    pe.wait_ge(den_read, it * NPAIR + p)
                late = {0: 0, 3: 0, 1: 1, 2: 1}
                for i, kts in enumerate(((0, 1), (3, 2))):
                    pe.wait_ge(masked1, (it * NPAIR + p) * NT + (2, 4)[i])
                    for kt in kts:
                        for j in range(2):
                            c0, row = segment(kt, j, 2), HD1 * late[kt] + 32 * j
                            last = mm(denB[row:row + 32, kt * P:S], ones[:, 0:32],
                                      wts[:, p % 2, c0:c0 + WIDTH[kt]], start=kt < 2, stop=kt >= 2)
                last.then_inc(den_done, 1)
                if p:
                    pe.wait_ge(num_read, it * NPAIR + p)
                for kt in (0, 1, 3, 2):
                    for j in range(2):
                        c0, hd = segment(kt, j, 2), 2 * p + j
                        last = mm(numB[HD1 * j:HD1 * j + HD1, kt * P:S], v1[:, kt, hd * HD1:(hd + 1) * HD1],
                                  wts[:, p % 2, c0:c0 + WIDTH[kt]], start=kt == 0, stop=kt == 2)
                last.then_inc(pv1_done, 1)

            def scale(it, p, step):
                pe.wait_ge(rrows_ready, it * NPAIR + p + 1)
                ps = fill(pe, Bh, it, step, "r")
                mm(ps[:, :], spread[:, :], rrows[:, :], start=True, stop=True).then_inc(Bh.filled, 1)

            def out1(it, n, step):
                pe.wait_ge(Bh.dve, drained(Bh, it, f"scale {NPAIR - 1}", "r"))
                ps = fill(pe, Bh, it, step, "y")
                for t in range(NT):
                    for p in range(NPAIR):
                        last = mm(ps[:, t * P:(t + 1) * P], yT[:, p, t * P:(t + 1) * P], wo1[:, p, :],
                                  start=p == 0, stop=p == NPAIR - 1)
                last.then_inc(Bh.filled, 1)

            fns = dict(norm=norm, up0=up0, down0=down0, qkv0=qkv0, shift=shift, exp=exp, pv0=pv0, turn=turn,
                       out0=out0, gates=gates, expert=expert, qkv1=qkv1, sq=sq, pv1=pv1, scale=scale,
                       out1=out1)
            fns["max"] = rowmax
            run(pe, fns)


def kernel(**inputs):
    import concourse.bacc as _bacc
    from concourse.bass_utils import run_bass_kernel_spmd as _run

    a = {k: np.asarray(v) for k, v in inputs.items()}
    rows = lambda m: np.ascontiguousarray(m)
    tiles = lambda m: rows(m.reshape(-1, P, m.shape[-1]).transpose(1, 0, 2))
    wv0 = a["L0_attn_Wv"].reshape(HD0, H0, D).transpose(1, 0, 2).reshape(D, D)
    weights = {
        "U1T": rows(a["L0_ffn_U1"].T), "V1": rows(a["L0_ffn_V1"]), "U2T": rows(a["L0_ffn_U2"].T),
        "V2": rows(a["L0_ffn_V2"]), "b1": rows(a["L0_ffn_b1"].reshape(NF, P).T),
        "b2": rows(np.broadcast_to(a["L0_ffn_b2"], (P, NT, D))),
        "wq0": rows(a["L0_attn_Wq"].T), "wk0": rows(a["L0_attn_Wk"].T), "wv0": rows(wv0.T),
        "wo0": rows(a["L0_attn_Wo"].T), "gb": rows(np.stack([a["L0_attn_gamma"], a["L0_attn_beta"]], 1)),
        "wq1": rows(a["L1_attn_Wq"].T), "wk1": rows(a["L1_attn_Wk"].T), "wv1": rows(a["L1_attn_Wv"].T),
        "wo1": tiles(a["L1_attn_Wo"].T), "rw": rows(a["L1_ffn_router_w"].T),
        "rbias": rows(np.broadcast_to(a["L1_ffn_router_bias"], (P, NT, NE))),
        "sw1": rows(a["L1_ffn_sw1"]), "sw3": rows(a["L1_ffn_sw3"]), "sw2": tiles(a["L1_ffn_sw2"]),
        "ew1": rows(a["L1_ffn_ew1"].transpose(1, 0, 2)), "ew2": rows(a["L1_ffn_ew2"].transpose(1, 0, 2)),
    }
    p, q = np.arange(P)[:, None], np.arange(P)[None, :]
    j = np.arange(GH)[None, :]
    consts = {
        "ident": (p == q), "negmask": np.where(q > p, MASKED, 0.0),
        "headmask": np.where(p < OFF_ROW, (p % 32) // HD0 == j, p == OFF_ROW + j),
        "spread": (p // 32 == q // HD1) & (p % 32 < 3),
        "pairmask": (p % 32) // FEAT == np.arange(2)[None, :],
        "iota8": np.broadcast_to(np.arange(NE), (P, NT, NE)),
    }
    consts = {k: np.ascontiguousarray(v, dtype=np.float32) for k, v in consts.items()}

    nc = _bacc.Bacc("TRN2", target_bir_lowering=False, num_devices=1)
    arrays = {"x_dram": rows(a["L0_attn_x"])}

    def dram(name, array):
        arrays[name] = array
        return nc.dram_tensor(name, array.shape, mybir.dt.from_np(array.dtype), kind="ExternalInput").ap()

    x_ap = dram("x_dram", arrays["x_dram"])
    w_aps = {k: dram(f"{k}_dram", v) for k, v in weights.items()}
    c_aps = {k: dram(f"{k}_const", v) for k, v in consts.items()}
    out_ap = nc.dram_tensor("out_dram", (B, S, D), F32, kind="ExternalOutput").ap()
    build_program(nc, x_ap, w_aps, c_aps, out_ap)
    r = _run(nc, [arrays], core_ids=[0])
    return r.results[0]["out_dram"]
```

```python
from contextlib import ExitStack

import numpy as np

import concourse.bass as bass
from concourse import mybir

F32 = mybir.dt.float32
F16 = mybir.dt.float16
BF16 = mybir.dt.bfloat16
U32 = mybir.dt.uint32
ALU = mybir.AluOpType
ACT = mybir.ActivationFunctionType
AX = mybir.AxisListType

B, S, D = 8, 512, 128
P = 128
NT = S // P
LN_EPS = 1e-5
F0, R0 = 512, 32
NF = F0 // P
H0, HD0 = 16, 8
GH = 4
NG = H0 // GH
VC = 32
OFF_ROW = 96
OFF_UNIT = 64.0
H1, FEAT, HD1 = 16, 16, 64
NPAIR = H1 // 2
TAYLOR_EPS = 1e-12
HS, HR, NE = 256, 128, 8
NS = HS // P
GATE_EPS = 1e-9
MASKED = -1e30

WIDTH = [S - P * kt for kt in range(NT)]


def segment(kt, head, heads):
    if kt == 0:
        return head * S
    if kt == 1:
        return (heads + head) * S
    if kt == 3:
        return (heads + head) * S + WIDTH[1]
    return 2 * heads * S + head * WIDTH[2]


def units_of(heads):
    return ([[(0, h)] for h in range(heads)] + [[(1, h), (3, h)] for h in range(heads)]
            + [[(2, h), (2, h + 1)] for h in range(0, heads, 2)])


UNITS0, UNITS1 = units_of(GH), units_of(2)
COLS0, COLS1 = len(UNITS0) * S, len(UNITS1) * S

CH0, CH1 = len(UNITS0) // 2, (len(UNITS1) + 1) // 2


def of_chunk(n, units):
    chunks = (len(units) + 1) // 2
    g, c = divmod(n, chunks)
    return g, list(range(2 * c, min(2 * c + 2, len(units)))), c == chunks - 1


def unit_step(name, g, u, units):
    return f"{name} {g * ((len(units) + 1) // 2) + u // 2}"


def chunks(name, g, n):
    return [f"{name} {g * n + c}" for c in range(n)]


ORDER_A = (["load", "stat 0", "norm 0", "up0 0", "up0 1", "down0 0", "stat 1", "norm 1", "qkv0", "pad0 0"]
           + chunks("max", 0, CH0) + ["pad0 1"] + chunks("max", 1, CH0) + ["shift 0", "pad0 2", "pad0 3"]
           + chunks("max", 2, CH0) + ["shift 1"] + chunks("exp", 0, CH0) + chunks("max", 3, CH0) + ["shift 2"]
           + chunks("exp", 1, CH0) + ["pv0 0", "shift 3"] + chunks("exp", 2, CH0) + ["turn 0", "pv0 1"]
           + chunks("exp", 3, CH0) + ["turn 1", "pv0 2", "turn 2", "pv0 3", "turn 3", "stat 2", "norm 2", "out0",
                                      "stat 3", "norm 3", "up0 2", "up0 3", "down0 1"])
MOE = [[f"router {n}", f"gate {NS * n}", f"gate {NS * n + 1}", f"route {n}"]
       + [f"expert {NE * n + e}" for e in range(NE)] for n in range(2)]
ORDER_B = (["take", "stat 0", "norm 0"] + MOE[0] + ["stat 1", "norm 1", "qk1"] + [f"v1 {t}" for t in range(NT)]
           + [f"pad1 {n}" for n in range(4)] + chunks("sq", 0, CH1) + chunks("sq", 1, CH1) + ["den 0", "num 0"]
           + [x for p in range(NPAIR - 2)
              for x in chunks("sq", p + 2, CH1) + [f"scale {p}", f"den {p + 1}", f"num {p + 1}"]]
           + [f"scale {NPAIR - 2}", f"den {NPAIR - 1}", f"num {NPAIR - 1}", f"scale {NPAIR - 1}", "out1", "stat 2",
              "norm 2"] + MOE[1] + ["store"])
DURATION = {"load": 1, "stat": 6, "norm": 1, "up0": 2, "down0": 4, "qkv0": 4, "pad0": 2, "max": 1.6, "shift": 2,
            "exp": 1.4, "pv0": 3, "turn": 1, "out0": 2, "take": 1, "router": 2, "gate": 3, "route": 1, "expert": 3,
            "qk1": 4, "v1": 2, "pad1": 1, "sq": 1.3, "den": 2, "num": 2, "scale": 1, "out1": 7, "store": 1}


def ring_uses(step):
    name, _, n = step.partition(" ")
    n = int(n or 0)
    if name == "norm":
        return [("lnT", "act")]
    if name == "up0":
        return [(f"up{f}", "act") for f in ((0, 1), (2, 3))[n % 2]]
    if name in ("down0", "out0", "out1"):
        return [("y", "dve")]
    if name == "qkv0":
        return [("q", "dve"), ("k", "dve"), ("v", "act")]
    if name == "max":
        return [(f"u{u}", "dve") for u in of_chunk(n, UNITS0)[1]]
    if name == "shift":
        return [("mT", "act")]
    if name == "exp":
        return [(f"u{u}", "act") for u in of_chunk(n, UNITS0)[1]]
    if name == "turn":
        return [("o", "dve")]
    if name == "router":
        return [("router", "act")]
    if name == "gate":
        return [("gate", "dve"), ("lin", "dve")]
    if name == "expert":
        e = n % NE
        return [(f"e{k}", "act") for k in ([0, 1] if e == 0 else [e + 1] if e + 1 < NE else [])]
    if name == "qk1":
        return [(f"{x}{t}", "dve") for x in "qk" for t in range(2)]
    if name == "v1":
        return [("low", "act"), ("high", "dve")]
    if name == "sq":
        return [(f"u{u}", "act") for u in of_chunk(n, UNITS1)[1]]
    if name == "scale":
        return [("r", "dve")]
    return []


def unit_of_expert(n, e):
    return f"expert {NE * n + max(e - 1, 0)}", f"e{e}"


def ring_table(order, banks):
    table, drained = {}, {"act": 0, "dve": 0}
    listed = [(step, u, e) for step in order for u, e in ring_uses(step)]
    for n, (step, u, e) in enumerate(listed):
        drained[e] += 1
        before = table[listed[n - banks][:2]] if n >= banks else None
        table[step, u] = Unit(n + 1, n % banks, e, drained[e], before)
    return table, Totals(len(listed), drained["act"], drained["dve"])


def weave(a, b):
    def stamped(order, half):
        total = sum(DURATION[s.split()[0]] for s in order)
        at, out = 0.0, []
        for s in order:
            out.append((at / total, half, s))
            at += DURATION[s.split()[0]]
        return out
    return [(h, s) for _, h, s in sorted(stamped(a, "A") + stamped(b, "B"), key=lambda x: x[0])]


class Unit:

    def __init__(self, n, bank, engine, count, before):
        self.n, self.bank, self.engine, self.count, self.before = n, bank, engine, count, before


class Totals:

    def __init__(self, filled, act, dve):
        self.filled, self.act, self.dve = filled, act, dve


class Half:
    pass


def bcast(ap, n):
    return bass.AP(ap.tensor, ap.offset, [list(x) for x in ap.ap[:-1]] + [[0, n]])


class Chain:

    def __init__(self, eng, sem, per):
        self.eng, self.sem, self.per, self.n, self.it = eng, sem, per, 0, 0

    def start(self, it):
        self.it, self.n = it, 0

    def then(self, ins, apart=None):
        self.n += 1
        ins.then_inc(self.sem, 1)
        self.eng.wait_ge(self.sem, self.it * self.per + self.n)
        if apart is not None:
            apart()

    def end(self):
        assert self.n == self.per, (self.n, self.per)


def build_program(nc, x, w, cst, out):
    ctx = ExitStack()
    with ctx:
        def sb(name, shape, dt=F32):
            return ctx.enter_context(nc.sbuf_tensor(name, shape, dt))

        def sem(name):
            return ctx.enter_context(nc.semaphore(name))

        banks = [ctx.enter_context(nc.psum_tensor(f"bank{i}", [P, S], F32)) for i in range(8)]
        ringA, accA = banks[0:3], banks[3]
        ringB, numB, denB = banks[4:6], banks[6], banks[7]
        TA, PERA = ring_table(ORDER_A, len(ringA))
        TB, PERB = ring_table(ORDER_B, len(ringB))

        ident = sb("ident", [P, P])
        identb = sb("identb", [P, P], BF16)
        negmask = sb("negmask", [P, P], BF16)
        headmask = sb("headmask", [P, GH])
        pairmask = sb("pairmask", [P, 2])
        iota8 = sb("iota8", [P, NT, NE])
        ones = sb("ones", [P, 32])
        spread = sb("spread", [P, P], BF16)
        neghalf = sb("neghalf", [P, NT])
        epsilon = sb("epsilon", [P, NT])
        spare_dve = sb("spare_dve", [1, 1])
        w1 = sb("w1", [P, F0])
        w2 = sb("w2", [P, NF, D])
        b1 = sb("b1", [P, NF]); b2h = sb("b2h", [P, NT, D])
        wq0 = sb("wq0", [P, D]); wk0 = sb("wk0", [P, D]); wv0 = sb("wv0", [P, D]); wo0 = sb("wo0", [P, D])
        gb = sb("gb", [P, 2])
        wq1 = sb("wq1", [P, H1 * FEAT]); wk1 = sb("wk1", [P, H1 * FEAT]); wv1 = sb("wv1", [P, H1 * HD1])
        wo1 = sb("wo1", [P, NPAIR, D])
        rw = sb("rw", [P, NE]); rbias = sb("rbias", [P, NT, NE])
        sw1 = sb("sw1", [P, HS]); sw3 = sb("sw3", [P, HS]); sw2 = sb("sw2", [P, NS, D])
        ew1 = sb("ew1", [P, NE, HR]); ew2 = sb("ew2", [P, NE, D])

        def half(name):
            h = Half()
            h.x = sb(f"x{name}", [P, NT, D])
            h.ln = sb(f"ln{name}", [P, NT, D])
            h.lnT = sb(f"lnT{name}", [P, S])
            h.stats, h.mv = sb(f"stats{name}", [P, NT, 6]), sb(f"mv{name}", [P, NT, 2])
            h.vare, h.rstd = sb(f"vare{name}", [P, NT]), sb(f"rstd{name}", [P, NT])
            h.spare = sb(f"spare{name}", [1, 1])
            h.filled = sem(f"filled{name}")
            h.act, h.dve = sem(f"drained_act{name}"), sem(f"drained_dve{name}")
            h.x_ready = sem(f"x_ready{name}")
            h.mv_ready, h.vare_ready = sem(f"mv_ready{name}"), sem(f"vare_ready{name}")
            h.rstd_ready, h.ln_ready = sem(f"rstd_ready{name}"), sem(f"ln_ready{name}")
            h.hi_ready = sem(f"hi_ready{name}")
            h.dve_step = sem(f"dve_step{name}")
            h.carried = sem(f"carried{name}")
            return h

        A, Bh = half("A"), half("B")
        A.ring, Bh.ring, A.T, Bh.T, A.per, Bh.per = ringA, ringB, TA, TB, PERA, PERB
        A.lns, Bh.lns = 4, 3
        A.carriers, Bh.carriers = 3 * NG, 3 * NPAIR
        A.name, Bh.name = "A", "B"
        probs = sb("probs", [P, 2, COLS0])
        hid0 = probs[:, 1, 0:NF * S].rearrange("p (f s) -> p f s", f=NF)
        p16 = probs[:, 0, :].bitcast(F16)
        q0h, q0l, k0h, k0l = (p16[:, i * S:(i + 1) * S] for i in range(4))
        kall = p16[:, 4 * S:(4 + NG) * S].rearrange("p (g s) -> p g s", g=NG)
        q0a = sb("q0a", [P, NG, S], F16)
        kpad0 = sb("kpad0", [P, H0, S], F16)
        vaug = sb("vaug", [P, NT, H0, HD0 + 1])
        bmax = sb("bmax", [P, len(UNITS0) * NT])
        rmax = sb("rmax", [P, NT, H0])
        offs = sb("offs", [GH, NG, S], F16)
        oT = sb("oT", [P, 2, S])
        rden = sb("rden", [P, NT, GH, 1])
        attn = sb("attn", [P, NT, D])
        mid = sb("mid", [P, NT, D])
        yT = sb("yT", [P, NPAIR, S])
        wts = sb("wts", [P, 2, COLS1])
        sgm, hsh, hexp = yT[:, 0:NS, :], yT[:, NS:2 * NS, :], yT[:, 2 * NS:2 * NS + 2, :]
        k1a = yT[0:96, 0:NPAIR // 2, :].rearrange("p a s -> p (a s)").bitcast(F16)\
            .rearrange("p (a s) -> p a s", s=S)
        w16 = wts[:, 0, :].bitcast(F16)
        q1h, q1l, k1h, k1l = (w16[:, 2 * i * S:2 * (i + 1) * S].rearrange("p (t s) -> p t s", t=2)
                              for i in range(4))
        U1T, V1 = wts[0:R0, 0, 0:D], wts[0:R0, 0, D:D + F0]
        U2T, V2 = wts[0:R0, 1, 0:F0], wts[0:R0, 1, F0:F0 + D]
        negf = wts[:, 1, F0 + D:F0 + D + P]
        spreadf = wts[:, 1, F0 + D + P:F0 + D + 2 * P]
        s8 = sb("s8", [P, NT, NE]); sel = sb("sel", [P, NT, NE]); top = sb("top", [P, NT, 8])
        idx = sb("idx", [P, NT, 8], U32); idf = sb("idf", [P, NT, 2])
        oh = sb("oh", [P, 2, NT, NE]); pick = sb("pick", [P, NT, NE]); ssel = sb("ssel", [P, NT, NE])
        den = sb("den", [P, NT, 1]); dsafe = sb("dsafe", [P, NT, 1]); half_if = sb("half_if", [P, NT, 1])
        rdn = sb("rdn", [P, NT, 1]); rsc = sb("rsc", [P, NT, 1]); flat = sb("flat", [P, NT, 1])
        gsc = sb("gsc", [P, NT, NE]); gfl = sb("gfl", [P, NT, NE]); comb = sb("comb", [P, NT, NE])
        acc = Bh.ln
        q1a = sb("q1a", [96, NPAIR, S], F16)
        kpad1 = sb("kpad1", [96, H1, S], F16)
        v1 = sb("v1", [P, NT, H1 * HD1])
        d32 = sb("d32", [P, S])
        dlate = sb("dlate", [HD1, S // 32]); dsum = sb("dsum", [HD1, S // 32]); rrec = sb("rrec", [HD1, S // 32])
        rrem = sb("rrem", [HD1, S // 32])
        rsplit = sb("rsplit", [P, S], BF16)
        rrows = sb("rrows", [P, S], BF16)
        res = sb("res", [P, NT, D])

        w_ready = sem("w_ready"); setup = sem("setup"); negb_ready = sem("negb_ready")
        offset_rows = sem("offset_rows")
        lowrank = sem("lowrank"); lowrank_copied = sem("lowrank_copied")
        qk0_laid = [sem(f"qk0_laid{g}") for g in range(NG)]
        qk1_laid = [sem(f"qk1_laid{n}") for n in range(4)]
        kpad0_ready = sem("kpad0_ready"); kpad1_ready = sem("kpad1_ready")
        rmax_ready = sem("rmax_ready"); offs_ready = sem("offs_ready")
        offs_laid = [sem(f"offs_laid{g}") for g in range(NG)]
        masked0 = sem("masked0"); pv0_done = sem("pv0_done"); oT_ready = sem("oT_ready")
        mid_taken = sem("mid_taken")
        gate_ready = sem("gate_ready"); hsh_ready = sem("hsh_ready")
        moe_out = sem("moe_out"); moe_added = sem("moe_added")
        plus1 = sem("plus1"); masked1 = sem("masked1"); pv1_done = sem("pv1_done")
        den_done = sem("den_done"); den_read = sem("den_read"); num_read = sem("num_read")
        rrows_ready = sem("rrows_ready")
        res_free = sem("res_free")

        NW = len(w)
        DVE_A, DVE_B = 10, 85
        QK_DMAS = 6
        order_loop = weave(ORDER_A, ORDER_B)

        def steps(fns, it_of, order):
            for h, step in order:
                name, _, n = step.partition(" ")
                if name in ("stat", "norm") and name in fns:
                    fns[name](A if h == "A" else Bh, it_of[h], int(n), step)
                elif name in fns:
                    fns[name](it_of[h], int(n or 0), step)

        def run(eng, fns, start=None, end=None):
            def part(it_of, order):
                if start:
                    start(it_of)
                steps(fns, it_of, order)
                if end:
                    end(it_of)
            part({"A": 0}, [("A", s) for s in ORDER_A])
            with eng.Fori(0, B - 1) as i:
                part({"A": i + 1, "B": i}, order_loop)
            part({"B": B - 1}, [("B", s) for s in ORDER_B])

        def fill(pe, h, it, step, unit):
            u = h.T[step, unit]
            if u.before:
                s = {"act": h.act, "dve": h.dve}[u.before.engine]
                pe.wait_ge(s, it * (h.per.act if u.before.engine == "act" else h.per.dve) + u.before.count)
            return h.ring[u.bank]

        def full(eng, h, it, step, unit):
            u = h.T[step, unit]
            eng.wait_ge(h.filled, it * h.per.filled + u.n)
            return h.ring[u.bank]

        def drained(h, it, step, unit):
            u = h.T[step, unit]
            return it * (h.per.act if u.engine == "act" else h.per.dve) + u.count

        block = ctx.enter_context(nc.Block())

        @block.sync
        def _(sp):
            for dst, src in ((ident[:], cst["ident"]), (negf, cst["negmask"]), (spreadf, cst["spread"]), (headmask[:], cst["headmask"]),
                             (pairmask[:], cst["pairmask"]), (iota8[:], cst["iota8"])):
                sp.dma_start(dst, src).then_inc(w_ready, 16)
            tiles = dict(U1T=U1T, V1=V1, U2T=U2T, V2=V2, b1=b1[:], b2=b2h[:], wq0=wq0[:], wk0=wk0[:], wv0=wv0[:], wo0=wo0[:],
                         gb=gb[:], wq1=wq1[:], wk1=wk1[:], wv1=wv1[:], wo1=wo1[:], rw=rw[:], rbias=rbias[:], sw1=sw1[:], sw3=sw3[:],
                         sw2=sw2[:], ew1=ew1[:], ew2=ew2[:])
            for name, src in w.items():
                sp.dma_start(tiles[name], src).then_inc(w_ready, 16)

            def load(it, _n, step):
                if not isinstance(it, int):
                    sp.wait_ge(A.dve, drained(A, it, "down0 1", "y") - A.per.dve)
                sp.dma_start(A.x[:, :, :], x[bass.ds(it, 1), :, :].rearrange("a (t p) d -> p (a t) d", p=P))\
                  .then_inc(A.x_ready, 16)

            def qkv0(it, _n, step):
                sp.wait_ge(A.dve, drained(A, it, step, "k"))
                for g in range(NG):
                    rows = slice(32 * g, 32 * g + 32)
                    for dst, parts in ((q0a, (q0h, q0h, q0l)), (kall, (k0h, k0l, k0h))):
                        for a, part in enumerate(parts):
                            sp.dma_start(dst[32 * a:32 * a + 32, g, :], part[rows, :]).then_inc(qk0_laid[g], 16)

            def shift(it, g, step):
                sp.wait_ge(A.act, drained(A, it, step, "mT"))
                sp.dma_start(q0a[OFF_ROW:OFF_ROW + GH, g, :], offs[:, g, :]).then_inc(offs_laid[g], 16)

            def qk1(it, _n, step):
                sp.wait_ge(Bh.dve, drained(Bh, it, step, "k1"))
                for n in range(4):
                    rows = slice(32 * n, 32 * n + 32)
                    for dst, parts in ((q1a, (q1h, q1h, q1l)), (k1a, (k1h, k1l, k1h))):
                        for a, part in enumerate(parts):
                            sp.dma_start(dst[32 * a:32 * a + 32, n:NPAIR:4, :], part[rows, :, :])\
                              .then_inc(qk1_laid[n], 16)

            def store(it, _n, step):
                sp.wait_ge(moe_added, (it * 2 + 2) * (NE + 1))
                sp.dma_start(out[bass.ds(it, 1), :, :].rearrange("a (t p) d -> p (a t) d", p=P), res[:, :, :])\
                  .then_inc(res_free, 16)

            run(sp, dict(load=load, qkv0=qkv0, shift=shift, qk1=qk1, store=store))
            sp.wait_ge(res_free, 16 * (B + 1))

        @block.gpsimd
        def _(pool):
            pool.memset(vaug[:, :, :, HD0:HD0 + 1], 1.0).then_inc(setup, 1)
            pool.memset(neghalf[:, :], -0.5).then_inc(setup, 1)
            pool.memset(epsilon[:, :], LN_EPS).then_inc(setup, 1)
            pool.memset(ones[:, :], 1.0).then_inc(setup, 1)
            pool.wait_ge(setup, 9)
            for h in (A, Bh):
                pool.tensor_tensor(h.spare[:, :], neghalf[0:1, 0:1], neghalf[0:1, 0:1], ALU.add).then_inc(h.carried, 1)

            def ln_scale(h, it, k, step):
                pool.wait_ge(h.mv_ready, it * h.lns + k + 1)
                pool.tensor_tensor(h.vare[:, :], h.mv[:, :, 1], epsilon[:, :], ALU.add).then_inc(h.vare_ready, 1)
                pool.wait_ge(h.vare_ready, it * h.lns + k + 1)
                pool.tensor_tensor(h.rstd[:, :], h.vare[:, :], neghalf[:, :], ALU.pow).then_inc(h.rstd_ready, 1)

            def wait_apart(h, it, n, sem, value):
                pool.wait_ge(h.carried, it * h.carriers + n + 1)
                pool.wait_ge(sem, value)
                pool.tensor_tensor(h.spare[:, :], neghalf[0:1, 0:1], neghalf[0:1, 0:1], ALU.add).then_inc(h.carried, 1)

            def mask(buf, heads, kt):
                step = {0: S, 1: S, 3: S, 2: WIDTH[2]}[kt]
                s0 = segment(kt, 0, heads)
                v = bass.AP(buf.tensor, buf.offset + s0, [list(buf.ap[0]), [step, heads], [1, P]])
                return pool.affine_select(out=v, in_=v, compare_op=ALU.is_ge, fill=0.0, base=0,
                                          pattern=[[0, heads], [1, P]], channel_multiplier=-1)

            def exp(it, n, step):
                g, units, _ = of_chunk(n, UNITS0)
                for kt, last in ((0, GH - 1), (1, 2 * GH - 1), (3, None), (2, len(UNITS0) - 1)):
                    if (last if last is not None else 2 * GH - 1) not in units:
                        continue
                    if last is not None:
                        wait_apart(A, it, g * 3 + (0, 1, 2)[kt], A.act, drained(A, it, step, f"u{last}"))
                    mask(probs[:, g % 2, :], GH, kt).then_inc(masked0, 1)

            def sq(it, n, step):
                wait_apart(Bh, it, n, plus1, it * NPAIR * CH1 + n + 1)
                for kt in ((0,), (1, 3), (2,))[n % CH1]:
                    mask(wts[:, n // CH1 % 2, :], 2, kt).then_inc(masked1, 1)

            run(pool, dict(stat=ln_scale, exp=exp, sq=sq))

        @block.scalar
        def _(act):
            act.wait_ge(w_ready, 16 * (NW + 6))
            act.activation(identb[:, :], ident[:, :], ACT.Copy).then_inc(negb_ready, 1)
            act.activation(negmask[:, :], negf[:, :], ACT.Copy).then_inc(negb_ready, 1)
            act.activation(spread[:, :], spreadf[:, :], ACT.Copy).then_inc(negb_ready, 1)
            act.wait_ge(lowrank, 1)
            act.activation(w1[:, :], ringA[0][:, :], ACT.Copy).then_inc(lowrank_copied, 1)
            act.activation(w2[:, :, :].rearrange("p a b -> p (a b)"), ringA[1][:, :], ACT.Copy)\
               .then_inc(lowrank_copied, 1)

            def norm(h, it, k, step):
                ps = full(act, h, it, step, "lnT")
                if h is A and k == 2:
                    act.activation(h.lnT[:, :], ps[:, :], ACT.Identity, bias=gb[:, 1:2], scale=gb[:, 0:1])\
                       .then_inc(h.act, 1)
                else:
                    act.activation(h.lnT[:, :], ps[:, :], ACT.Copy).then_inc(h.act, 1)

            def up0(it, n, step):
                for unit, _ in ring_uses(step):
                    f = int(unit[2:])
                    ps = full(act, A, it, step, unit)
                    act.activation(hid0[:, f, :], ps[:, :], ACT.Gelu_apprx_tanh, bias=b1[:, f:f + 1])\
                       .then_inc(A.act, 1)

            def qkv0(it, n, step):
                ps = full(act, A, it, step, "q")
                act.activation(q0h[:, :], ps[:, :], ACT.Copy).then_inc(A.hi_ready, 1)
                ps = full(act, A, it, step, "k")
                act.activation(k0h[:, :], ps[:, :], ACT.Copy, scale=HD0 ** -0.5).then_inc(A.hi_ready, 1)
                ps = full(act, A, it, step, "v")
                act.wait_ge(setup, 9)
                act.activation(vaug[:, :, :, 0:HD0].rearrange("p t h d -> p (t h) d"),
                               ps[:, :].rearrange("p (a d) -> p a d", d=HD0), ACT.Copy).then_inc(A.act, 1)

            def shift(it, g, step):
                ps = full(act, A, it, step, "mT")
                act.activation(offs[:, g, :], ps[0:GH, :], ACT.Copy, scale=-1.0 / OFF_UNIT).then_inc(A.act, 1)

            def exp(it, n, step):
                g, units, _ = of_chunk(n, UNITS0)
                if n == 0:
                    act.wait_ge(kpad0_ready, it * NG + NG)
                if g >= 2 and 0 in units:
                    act.wait_ge(pv0_done, it * NG + g - 1)
                for u in units:
                    ps = full(act, A, it, step, f"u{u}")
                    act.activation(probs[:, g % 2, u * S:(u + 1) * S], ps[:, :], ACT.Exp).then_inc(A.act, 1)

            def router(it, n, step):
                ps = full(act, Bh, it, step, "router")
                act.activation(s8[:, :, :].rearrange("p t e -> p (t e)"), ps[:, 0:NT * NE], ACT.Sigmoid)\
                   .then_inc(Bh.act, 1)

            def gate(it, n, step):
                ps = full(act, Bh, it, step, "gate")
                act.activation(sgm[:, n % NS, :], ps[:, :], ACT.Sigmoid).then_inc(gate_ready, 1)

            def expert(it, n, step):
                for unit, _ in ring_uses(step):
                    e = int(unit[1:])
                    ps = full(act, Bh, it, step, unit)
                    if e >= 2:
                        act.wait_ge(moe_out, (it * 2 + n // NE) * (NE + 1) + 1 + e - 1)
                    act.activation(hexp[:, e % 2, :], ps[:, :], ACT.Gelu).then_inc(Bh.act, 1)

            def qk1(it, n, step):
                for name, hi in (("q", q1h), ("k", k1h)):
                    for t in range(2):
                        ps = full(act, Bh, it, step, f"{name}{t}")
                        act.activation(hi[:, t, :], ps[:, :], ACT.Copy).then_inc(Bh.hi_ready, 1)

            def values1(it, t, step):
                ps = full(act, Bh, it, step, "low")
                act.activation(v1[:, t, 0:S], ps[:, :], ACT.Copy).then_inc(Bh.act, 1)

            def sq(it, n, step):
                p, units, _ = of_chunk(n, UNITS1)
                if n == 0:
                    act.wait_ge(kpad1_ready, it * 4 + 4)
                if p >= 2 and 0 in units:
                    act.wait_ge(pv1_done, it * NPAIR + p - 1)
                for u in units:
                    ps = full(act, Bh, it, step, f"u{u}")
                    act.activation(wts[:, p % 2, u * S:(u + 1) * S], ps[:, :], ACT.Square,
                                   bias=1.0, scale=FEAT ** -0.5).then_inc(Bh.act, 1)

            def num(it, p, step):
                act.wait_ge(pv1_done, it * NPAIR + p + 1)
                act.activation(yT[:, p, :], numB[:, :], ACT.Copy).then_inc(num_read, 1)

            fns = dict(norm=norm, up0=up0, qkv0=qkv0, shift=shift, exp=exp, router=router, gate=gate, expert=expert,
                       qk1=qk1, v1=values1, sq=sq, num=num)
            run(act, fns)

        @block.vector
        def _(dve):
            def carrier():
                dve.memset(spare_dve[:, :], 0.0)

            chA, chB = Chain(dve, A.dve_step, DVE_A), Chain(dve, Bh.dve_step, DVE_B)
            dve.wait_ge(w_ready, 16 * (NW + 6))
            dve.tensor_scalar(b2h[:, :, :], b2h[:, :, :], 0.5, None, ALU.mult).then_inc(setup, 1)
            dve.memset(accA[:, :], 0.0).then_inc(setup, 1)
            dve.memset(rsplit[:, :], 0.0).then_inc(setup, 1)
            dve.memset(dlate[:, :], 0.0).then_inc(setup, 1)
            dve.memset(q0a[OFF_ROW:P, :, :], 0.0).then_inc(setup, 1)
            dve.memset(kpad0[OFF_ROW:P, :, :], OFF_UNIT).then_inc(offset_rows, 1)
            dve.wait_ge(offset_rows, 1)
            for hd in range(H0):
                dve.tensor_scalar(kpad0[OFF_ROW:P, hd, :], kpad0[OFF_ROW:P, hd, :],
                                  headmask[OFF_ROW:P, hd % GH:hd % GH + 1], None, ALU.mult)
            dve.memset(res[:, :, :], 0.0).then_inc(res_free, 16)
            dve.wait_ge(setup, 9)

            def stat(h, it, k, step):
                ch, src = (chA, attn if k == 2 else A.x) if h is A else (chB, Bh.x)
                if h is A and k == 0:
                    dve.wait_ge(A.x_ready, (it + 1) * 16)
                elif h is A:
                    before = {1: ("down0 0", "y"), 2: (f"turn {NG - 1}", "o"), 3: ("out0", "y")}[k]
                    dve.wait_ge(A.dve, drained(A, it, *before))
                elif k == 0:
                    dve.wait_ge(mid_taken, it + 1)
                elif k == 1:
                    dve.wait_ge(moe_added, (it * 2 + 1) * (NE + 1))
                else:
                    dve.wait_ge(Bh.dve, drained(Bh, it, "out1", "y"))
                for t in range(NT):
                    last = dve.bn_stats(h.stats[:, t, :], src[:, t, :])
                ch.then(last, carrier)
                for t in range(NT):
                    last = dve.bn_aggr(h.mv[:, t, :], h.stats[:, t, :])
                last.then_inc(h.mv_ready, 1)
                dve.wait_ge(h.rstd_ready, it * h.lns + k + 1)
                for t in range(NT):
                    last = dve.tensor_scalar(h.ln[:, t, :], src[:, t, :], h.mv[:, t, 0:1], h.rstd[:, t:t + 1],
                                             ALU.subtract, ALU.mult)
                last.then_inc(h.ln_ready, 1)

            def down0(it, n, step):
                full(dve, A, it, f"norm {(0, 3)[n]}", "lnT")
                chA.then(dve.tensor_tensor(A.ln[:, :, :], A.x[:, :, :], b2h[:, :, :], ALU.add))
                ps = full(dve, A, it, step, "y")
                dst = A.x if n == 0 else mid
                if n == 1 and not isinstance(it, int):
                    dve.wait_ge(mid_taken, it)
                dve.scalar_tensor_tensor(out=dst[:, :, :].rearrange("p t d -> p (t d)"), in0=ps[:, :],
                                         scalar=0.5, in1=A.ln[:, :, :].rearrange("p t d -> p (t d)"),
                                         op0=ALU.mult, op1=ALU.add).then_inc(A.dve, 1)

            def qkv0(it, n, step):
                for i, (name, hi, lo, sc) in enumerate((("q", q0h, q0l, 1.0), ("k", k0h, k0l, HD0 ** -0.5))):
                    ps = full(dve, A, it, step, name)
                    dve.wait_ge(A.hi_ready, it * 2 + i + 1)
                    dve.scalar_tensor_tensor(out=lo[:, :], in0=ps[:, :], scalar=sc, in1=hi[:, :],
                                             op0=ALU.mult, op1=ALU.subtract).then_inc(A.dve, 1)

            def pad0(it, g, step):
                dve.wait_ge(qk0_laid[g], (it + 1) * 16 * QK_DMAS)
                dve.memset(q0a[OFF_ROW:P, g, :], 0.0)
                for hd in range(GH * g, GH * g + GH):
                    last = dve.tensor_scalar(kpad0[0:OFF_ROW, hd, :], kall[0:OFF_ROW, g, :],
                                             headmask[0:OFF_ROW, hd % GH:hd % GH + 1], None, ALU.mult)
                last.then_inc(kpad0_ready, 1)

            def rowmax(it, n, step):
                g, units, last = of_chunk(n, UNITS0)
                for u in units:
                    ps = full(dve, A, it, step, f"u{u}")
                    dve.tensor_reduce(bmax[:, u * NT:(u + 1) * NT], ps[:, :].rearrange("p (b k) -> p b k", k=P),
                                      AX.X, ALU.max).then_inc(A.dve, 1)
                if not last:
                    return
                dve.wait_ge(A.dve, drained(A, it, step, f"u{len(UNITS0) - 1}"))
                heads = slice(g * GH, (g + 1) * GH)
                wide = bmax[:, 0:GH * NT].rearrange("p (h b) -> p h b", b=NT)
                pair = bmax[:, GH * NT:2 * GH * NT].rearrange("p (h b) -> p h b", b=NT)
                two = bmax[:, 2 * GH * NT:].rearrange("p (h b) -> p h b", b=2)
                dve.tensor_reduce(rmax[:, 3, heads], wide, AX.X, ALU.max)
                dve.tensor_reduce(rmax[:, 2, heads], pair[:, :, 0:3], AX.X, ALU.max)
                dve.tensor_reduce(rmax[:, 1, heads], two, AX.X, ALU.max)
                dve.tensor_reduce(rmax[:, 0, heads], pair[:, :, 3:4], AX.X, ALU.max).then_inc(rmax_ready, 1)
                dve.wait_ge(rmax_ready, it * NG + g + 1)

            def pv0(it, g, step):
                dve.wait_ge(pv0_done, it * NG + g + 1)
                dve.tensor_copy(oT[:, g % 2, :], accA[:, :]).then_inc(oT_ready, 1)

            def turn(it, g, step):
                ps = full(dve, A, it, step, "o")
                v = ps[:, :].rearrange("p (t h c) -> p t h c", t=NT, c=VC)
                chA.then(dve.reciprocal(rden[:, :, :, :], v[:, :, :, HD0:HD0 + 1]))
                dst = attn[:, :, g * GH * HD0:(g + 1) * GH * HD0].rearrange("p t (h c) -> p t h c", c=HD0)
                dve.tensor_tensor(dst, v[:, :, :, 0:HD0], bcast(rden[:, :, :, :], HD0), ALU.mult)\
                   .then_inc(A.dve, 1)

            def out0(it, n, step):
                ps = full(dve, A, it, step, "y")
                dve.tensor_tensor(A.x[:, :, :].rearrange("p t d -> p (t d)"), ps[:, :],
                                  A.x[:, :, :].rearrange("p t d -> p (t d)"), ALU.add).then_inc(A.dve, 1)

            def take(it, n, step):
                dve.wait_ge(A.dve, drained(A, it, "down0 1", "y"))
                dve.tensor_copy(Bh.x[:, :, :], mid[:, :, :]).then_inc(mid_taken, 1)

            def route(it, n, step):
                c = chB
                dve.wait_ge(Bh.act, drained(Bh, it, f"router {n}", "router"))
                c.then(dve.tensor_tensor(sel[:, :, :], s8[:, :, :], rbias[:, :, :], ALU.add), carrier)
                for t in range(NT):
                    last = dve.max(top[:, t, :], sel[:, t, :])
                c.then(last, carrier)
                for t in range(NT):
                    last = dve.max_index(idx[:, t, :], top[:, t, :], sel[:, t, :])
                c.then(last)
                c.then(dve.tensor_copy(idf[:, :, :], idx[:, :, 0:2]))
                for j in range(2):
                    last = dve.tensor_tensor(oh[:, j, :, :], iota8[:, :, :], bcast(idf[:, :, j:j + 1], NE),
                                             ALU.is_equal)
                c.then(last)
                c.then(dve.tensor_tensor(pick[:, :, :], oh[:, 0, :, :], oh[:, 1, :, :], ALU.add))
                c.then(dve.tensor_tensor(ssel[:, :, :], s8[:, :, :], pick[:, :, :], ALU.mult))
                c.then(dve.tensor_reduce(den[:, :, :], ssel[:, :, :], AX.X, ALU.add))
                dve.tensor_scalar(dsafe[:, :, :], den[:, :, :], GATE_EPS, None, ALU.add)
                c.then(dve.tensor_scalar(half_if[:, :, :], den[:, :, :], GATE_EPS, 0.5, ALU.is_gt, ALU.mult))
                c.then(dve.reciprocal(rdn[:, :, :], dsafe[:, :, :]))
                dve.tensor_scalar(flat[:, :, :], half_if[:, :, :], -0.5, 0.25, ALU.mult, ALU.add)
                c.then(dve.tensor_tensor(rsc[:, :, :], rdn[:, :, :], half_if[:, :, :], ALU.mult))
                dve.tensor_tensor(gsc[:, :, :], ssel[:, :, :], bcast(rsc[:, :, :], NE), ALU.mult)
                c.then(dve.tensor_tensor(gfl[:, :, :], pick[:, :, :], bcast(flat[:, :, :], NE), ALU.mult))
                c.then(dve.tensor_tensor(comb[:, :, :], gsc[:, :, :], gfl[:, :, :], ALU.add))

            def gate(it, nf, step):
                f = nf % NS
                ps = full(dve, Bh, it, step, "gate")
                dve.wait_ge(gate_ready, it * 2 * NS + nf + 1)
                dve.tensor_tensor(sgm[:, f, :], ps[:, :], sgm[:, f, :], ALU.mult).then_inc(Bh.dve, 1)
                dve.wait_ge(Bh.dve, drained(Bh, it, step, "gate"))
                ps = full(dve, Bh, it, step, "lin")
                dve.tensor_tensor(hsh[:, f, :], ps[:, :], sgm[:, f, :], ALU.mult).then_inc(Bh.dve, 1)

            def expert(it, ne, step):
                n, e = ne // NE, ne % NE
                first = (it * 2 + n) * (NE + 1)
                if e == 0:
                    dve.wait_ge(moe_out, first + 1)
                    dve.scalar_tensor_tensor(out=acc[:, :, :].rearrange("p t d -> p (t d)"), in0=numB[:, :],
                                             scalar=0.5, in1=Bh.x[:, :, :].rearrange("p t d -> p (t d)"),
                                             op0=ALU.mult, op1=ALU.add).then_inc(moe_added, 1)
                dve.wait_ge(moe_out, first + 2 + e)
                dve.wait_ge(moe_added, first + 1 + e)
                ps, dst = (denB, numB)[e % 2], acc
                if e == NE - 1:
                    dst = (Bh.x, res)[n]
                    if n == 1:
                        dve.wait_ge(res_free, 16 * (it + 1))
                for t in range(NT):
                    last = dve.scalar_tensor_tensor(out=dst[:, t, :], in0=ps[:, t * P:(t + 1) * P],
                                                    scalar=comb[:, t, e:e + 1], in1=acc[:, t, :],
                                                    op0=ALU.mult, op1=ALU.add)
                last.then_inc(moe_added, 1)

            def qk1(it, n, step):
                for i, (name, t, hi, lo) in enumerate((("q", 0, q1h, q1l), ("q", 1, q1h, q1l),
                                                       ("k", 0, k1h, k1l), ("k", 1, k1h, k1l))):
                    ps = full(dve, Bh, it, step, f"{name}{t}")
                    dve.wait_ge(Bh.hi_ready, it * 4 + i + 1)
                    dve.tensor_tensor(lo[:, t, :], ps[:, :], hi[:, t, :], ALU.subtract).then_inc(Bh.dve, 1)

            def values1(it, t, step):
                ps = full(dve, Bh, it, step, "high")
                dve.tensor_copy(v1[:, t, S:2 * S], ps[:, :]).then_inc(Bh.dve, 1)

            def pad1(it, n, step):
                dve.wait_ge(qk1_laid[n], (it + 1) * 16 * QK_DMAS)
                for hd in (2 * n, 2 * n + 1, 2 * n + 8, 2 * n + 9):
                    last = dve.tensor_scalar(kpad1[:, hd, :], k1a[:, hd // 2, :], pairmask[0:96, hd % 2:hd % 2 + 1],
                                             None, ALU.mult)
                last.then_inc(kpad1_ready, 1)

            def sq(it, n, step):
                p, units, _ = of_chunk(n, UNITS1)
                dve.wait_ge(Bh.act, drained(Bh, it, step, f"u{units[-1]}"))
                v = wts[:, p % 2, units[0] * S:(units[-1] + 1) * S]
                dve.tensor_scalar(v, v, 1.0, None, ALU.add).then_inc(plus1, 1)

            def den1(it, p, step):
                dve.wait_ge(den_done, it * NPAIR + p + 1)
                dve.transpose(d32[:, :], denB[:, :]).then_inc(den_read, 1)
                dve.wait_ge(den_read, it * NPAIR + p + 1)
                v = d32[:, :].rearrange("p (b c) -> p b c", c=32)
                part = rsplit[0:HD1, :].rearrange("p (b c) -> p b c", c=32)
                nb = P // 32
                chB.then(dve.tensor_copy(dlate[:, nb:], v[HD1:P, nb:, 0]))
                chB.then(dve.scalar_tensor_tensor(out=dsum[:, :], in0=v[0:HD1, :, 0], scalar=2 * TAYLOR_EPS,
                                                  in1=dlate[:, :], op0=ALU.add, op1=ALU.add))
                chB.then(dve.reciprocal(rrec[:, :], dsum[:, :]))
                chB.then(dve.tensor_copy(part[:, :, 0], rrec[:, :]))
                chB.then(dve.tensor_tensor(rrem[:, :], rrec[:, :], part[:, :, 0], ALU.subtract))
                chB.then(dve.tensor_copy(part[:, :, 1], rrem[:, :]))
                chB.then(dve.tensor_tensor(part[:, :, 2], rrem[:, :], part[:, :, 1], ALU.subtract))
                dve.transpose(rrows[:, :], rsplit[:, :]).then_inc(rrows_ready, 1)

            def scale(it, p, step):
                ps = full(dve, Bh, it, step, "r")
                dve.wait_ge(num_read, it * NPAIR + p + 1)
                dve.tensor_tensor(yT[:, p, :], ps[:, :], yT[:, p, :], ALU.mult).then_inc(Bh.dve, 1)

            def out1(it, n, step):
                ps = full(dve, Bh, it, step, "y")
                dve.tensor_tensor(Bh.x[:, :, :].rearrange("p t d -> p (t d)"), ps[:, :],
                                  Bh.x[:, :, :].rearrange("p t d -> p (t d)"), ALU.add).then_inc(Bh.dve, 1)

            def start(it_of):
                for h, ch in (("A", chA), ("B", chB)):
                    if h in it_of:
                        ch.start(it_of[h])

            def end(it_of):
                for h, ch in (("A", chA), ("B", chB)):
                    if h in it_of:
                        ch.end()

            fns = dict(stat=stat, down0=down0, qkv0=qkv0, pad0=pad0, pv0=pv0, turn=turn, out0=out0, take=take,
                       route=route, gate=gate, expert=expert, qk1=qk1, v1=values1, pad1=pad1, sq=sq, den=den1,
                       scale=scale, out1=out1)
            fns["max"] = rowmax
            run(dve, fns, start, end)

        @block.tensor
        def _(pe):
            mm = nc.tensor.matmul
            pe.wait_ge(w_ready, 16 * (NW + 6))
            mm(ringA[0][:, :], U1T[:, :], V1[:, :], start=True, stop=True)
            for f in range(NF):
                last = mm(ringA[1][:, f * D:(f + 1) * D], U2T[:, f * P:(f + 1) * P], V2[:, :], start=True, stop=True)
            last.then_inc(lowrank, 1)
            pe.wait_ge(lowrank_copied, 2)
            pe.wait_ge(negb_ready, 3)
            pe.wait_ge(setup, 9)

            def norm(h, it, k, step):
                pe.wait_ge(h.ln_ready, it * h.lns + k + 1)
                ps = fill(pe, h, it, step, "lnT")
                for t in range(NT):
                    last = nc.tensor.transpose(ps[:, t * P:(t + 1) * P], h.ln[:, t, :], ident[:, :])
                last.then_inc(h.filled, 1)

            def up0(it, n, step):
                pe.wait_ge(A.act, drained(A, it, f"norm {(0, 3)[n // 2]}", "lnT"))
                for unit, _ in ring_uses(step):
                    f = int(unit[2:])
                    ps = fill(pe, A, it, step, unit)
                    mm(ps[:, :], w1[:, f * P:(f + 1) * P], A.lnT[:, :], start=True, stop=True).then_inc(A.filled, 1)

            def down0(it, n, step):
                ps = fill(pe, A, it, step, "y")
                pe.wait_ge(A.act, drained(A, it, f"up0 {2 * n + 1}", f"up{NF - 1}"))
                for t in range(NT):
                    for f in range(NF):
                        last = mm(ps[:, t * P:(t + 1) * P], hid0[:, f, t * P:(t + 1) * P], w2[:, f, :],
                                  start=f == 0, stop=f == NF - 1)
                last.then_inc(A.filled, 1)

            def qkv0(it, n, step):
                pe.wait_ge(A.act, drained(A, it, "norm 1", "lnT"))
                for name, wt in (("q", wq0), ("k", wk0)):
                    ps = fill(pe, A, it, step, name)
                    mm(ps[:, :], wt[:, :], A.lnT[:, :], start=True, stop=True).then_inc(A.filled, 1)
                ps = fill(pe, A, it, step, "v")
                for t in range(NT):
                    last = mm(ps[:, t * P:(t + 1) * P], A.lnT[:, t * P:(t + 1) * P], wv0[:, :], start=True, stop=True)
                last.then_inc(A.filled, 1)

            def rowmax(it, n, step):
                g, units, _ = of_chunk(n, UNITS0)
                pe.wait_ge(kpad0_ready, it * NG + g + 1)
                for u in units:
                    ps = fill(pe, A, it, step, f"u{u}")
                    for kt, j in UNITS0[u]:
                        qt, c0 = NT - 1 - kt, segment(kt, j, GH) - u * S
                        n_keys = (qt + 1) * P
                        mm(ps[:, c0:c0 + n_keys], q0a[:, g, qt * P:(qt + 1) * P],
                           kpad0[:, g * GH + j, 0:n_keys], start=True, stop=False)
                        last = mm(ps[:, c0 + n_keys - P:c0 + n_keys], identb[:, :], negmask[:, :],
                                  start=False, stop=True)
                    last.then_inc(A.filled, 1)

            def shift(it, g, step):
                pe.wait_ge(rmax_ready, it * NG + g + 1)
                ps = fill(pe, A, it, step, "mT")
                for t in range(NT):
                    last = nc.tensor.transpose(ps[0:GH, t * P:(t + 1) * P], rmax[:, t, g * GH:(g + 1) * GH],
                                               ident[:, :])
                last.then_inc(A.filled, 1)

            def exp(it, n, step):
                g, units, _ = of_chunk(n, UNITS0)
                pe.wait_ge(offs_laid[g], (it + 1) * 16)
                for u in units:
                    ps = fill(pe, A, it, step, f"u{u}")
                    for kt, j in UNITS0[u]:
                        c0 = segment(kt, j, GH) - u * S
                        last = mm(ps[:, c0:c0 + WIDTH[kt]], kpad0[:, g * GH + j, kt * P:(kt + 1) * P],
                                  q0a[:, g, kt * P:S], start=True, stop=True)
                    last.then_inc(A.filled, 1)

            def pv0(it, g, step):
                if g:
                    pe.wait_ge(oT_ready, it * NG + g)
                for i, kt in enumerate((0, 1, 3, 2)):
                    pe.wait_ge(masked0, it * NG * NT + g * NT + i + 1)
                    for j in range(GH):
                        c0 = segment(kt, j, GH)
                        last = mm(accA[VC * j:VC * j + HD0 + 1, kt * P:S], vaug[:, kt, g * GH + j, :],
                                  probs[:, g % 2, c0:c0 + WIDTH[kt]], start=kt == 0, stop=kt == 2)
                last.then_inc(pv0_done, 1)

            def turn(it, g, step):
                pe.wait_ge(oT_ready, it * NG + g + 1)
                ps = fill(pe, A, it, step, "o")
                for t in range(NT):
                    last = nc.tensor.transpose(ps[:, t * P:(t + 1) * P], oT[:, g % 2, t * P:(t + 1) * P], ident[:, :])
                last.then_inc(A.filled, 1)

            def out0(it, n, step):
                pe.wait_ge(A.act, drained(A, it, "norm 2", "lnT"))
                ps = fill(pe, A, it, step, "y")
                for t in range(NT):
                    last = mm(ps[:, t * P:(t + 1) * P], A.lnT[:, t * P:(t + 1) * P], wo0[:, :], start=True, stop=True)
                last.then_inc(A.filled, 1)

            def router(it, n, step):
                pe.wait_ge(Bh.act, drained(Bh, it, f"norm {(0, 2)[n]}", "lnT"))
                ps = fill(pe, Bh, it, step, "router")
                for t in range(NT):
                    last = mm(ps[:, t * NE:(t + 1) * NE], Bh.lnT[:, t * P:(t + 1) * P], rw[:, :], start=True, stop=True)
                last.then_inc(Bh.filled, 1)

            def gate(it, nf, step):
                f = nf % NS
                for unit, wt in (("gate", sw1), ("lin", sw3)):
                    ps = fill(pe, Bh, it, step, unit)
                    mm(ps[:, :], wt[:, f * P:(f + 1) * P], Bh.lnT[:, :], start=True, stop=True).then_inc(Bh.filled, 1)

            def expert(it, ne, step):
                n, e = ne // NE, ne % NE
                first = (it * 2 + n) * (NE + 1)
                for unit, _ in ring_uses(step):
                    ps = fill(pe, Bh, it, step, unit)
                    mm(ps[:, :], ew1[:, int(unit[1:]), :], Bh.lnT[:, :], start=True, stop=True).then_inc(Bh.filled, 1)
                if e == 0:
                    pe.wait_ge(Bh.dve, drained(Bh, it, f"gate {n * NS + NS - 1}", "lin"))
                    for t in range(NT):
                        for f in range(NS):
                            last = mm(numB[:, t * P:(t + 1) * P], hsh[:, f, t * P:(t + 1) * P], sw2[:, f, :],
                                      start=f == 0, stop=f == NS - 1)
                    last.then_inc(moe_out, 1)
                else:
                    pe.wait_ge(moe_added, first + e)
                pe.wait_ge(Bh.act, drained(Bh, it, *unit_of_expert(n, e)))
                ps = (denB, numB)[e % 2]
                for t in range(NT):
                    last = mm(ps[:, t * P:(t + 1) * P], hexp[:, e % 2, t * P:(t + 1) * P], ew2[:, e, :],
                              start=True, stop=True)
                last.then_inc(moe_out, 1)

            def qk1(it, n, step):
                pe.wait_ge(Bh.act, drained(Bh, it, "norm 1", "lnT"))
                for name, wt in (("q", wq1), ("k", wk1)):
                    for t in range(2):
                        ps = fill(pe, Bh, it, step, f"{name}{t}")
                        mm(ps[:, :], wt[:, t * P:(t + 1) * P], Bh.lnT[:, :], start=True, stop=True)\
                            .then_inc(Bh.filled, 1)

            def values1(it, t, step):
                for c, unit in enumerate(("low", "high")):
                    ps = fill(pe, Bh, it, step, unit)
                    mm(ps[:, :], Bh.lnT[:, t * P:(t + 1) * P], wv1[:, c * S:(c + 1) * S], start=True, stop=True)\
                        .then_inc(Bh.filled, 1)

            def sq(it, n, step):
                p, units, _ = of_chunk(n, UNITS1)
                if p < 4 and 0 in units:
                    pe.wait_ge(kpad1_ready, it * 4 + p + 1)
                for u in units:
                    ps = fill(pe, Bh, it, step, f"u{u}")
                    for kt, j in UNITS1[u]:
                        c0 = segment(kt, j, 2) - u * S
                        last = mm(ps[:, c0:c0 + WIDTH[kt]], kpad1[:, 2 * p + j, kt * P:(kt + 1) * P],
                                  q1a[:, p, kt * P:S], start=True, stop=True)
                    last.then_inc(Bh.filled, 1)

            def den1(it, p, step):
                if p:
                    pe.wait_ge(den_read, it * NPAIR + p)
                late = {0: 0, 3: 0, 1: 1, 2: 1}
                for i, kts in enumerate(((0, 1), (3, 2))):
                    pe.wait_ge(masked1, (it * NPAIR + p) * NT + (2, 4)[i])
                    for kt in kts:
                        for j in range(2):
                            c0, row = segment(kt, j, 2), HD1 * late[kt] + 32 * j
                            last = mm(denB[row:row + 32, kt * P:S], ones[:, 0:32],
                                      wts[:, p % 2, c0:c0 + WIDTH[kt]], start=kt < 2, stop=kt >= 2)
                last.then_inc(den_done, 1)

            def num(it, p, step):
                if p:
                    pe.wait_ge(num_read, it * NPAIR + p)
                for kt in (0, 1, 3, 2):
                    for j in range(2):
                        c0, hd = segment(kt, j, 2), 2 * p + j
                        last = mm(numB[HD1 * j:HD1 * j + HD1, kt * P:S], v1[:, kt, hd * HD1:(hd + 1) * HD1],
                                  wts[:, p % 2, c0:c0 + WIDTH[kt]], start=kt == 0, stop=kt == 2)
                last.then_inc(pv1_done, 1)

            def scale(it, p, step):
                pe.wait_ge(rrows_ready, it * NPAIR + p + 1)
                ps = fill(pe, Bh, it, step, "r")
                mm(ps[:, :], spread[:, :], rrows[:, :], start=True, stop=True).then_inc(Bh.filled, 1)

            def out1(it, n, step):
                pe.wait_ge(Bh.dve, drained(Bh, it, f"scale {NPAIR - 1}", "r"))
                ps = fill(pe, Bh, it, step, "y")
                for t in range(NT):
                    for p in range(NPAIR):
                        last = mm(ps[:, t * P:(t + 1) * P], yT[:, p, t * P:(t + 1) * P], wo1[:, p, :],
                                  start=p == 0, stop=p == NPAIR - 1)
                last.then_inc(Bh.filled, 1)

            fns = dict(norm=norm, up0=up0, down0=down0, qkv0=qkv0, shift=shift, exp=exp, pv0=pv0, turn=turn,
                       out0=out0, router=router, gate=gate, expert=expert, qk1=qk1, v1=values1, sq=sq, den=den1,
                       num=num, scale=scale, out1=out1)
            fns["max"] = rowmax
            run(pe, fns)


def kernel(**inputs):
    import concourse.bacc as _bacc
    from concourse.bass_utils import run_bass_kernel_spmd as _run

    a = {k: np.asarray(v) for k, v in inputs.items()}
    rows = lambda m: np.ascontiguousarray(m)
    tiles = lambda m: rows(m.reshape(-1, P, m.shape[-1]).transpose(1, 0, 2))
    wv0 = a["L0_attn_Wv"].reshape(HD0, H0, D).transpose(1, 0, 2).reshape(D, D)
    weights = {
        "U1T": rows(a["L0_ffn_U1"].T), "V1": rows(a["L0_ffn_V1"]), "U2T": rows(a["L0_ffn_U2"].T),
        "V2": rows(a["L0_ffn_V2"]), "b1": rows(a["L0_ffn_b1"].reshape(NF, P).T),
        "b2": rows(np.broadcast_to(a["L0_ffn_b2"], (P, NT, D))),
        "wq0": rows(a["L0_attn_Wq"].T), "wk0": rows(a["L0_attn_Wk"].T), "wv0": rows(wv0.T),
        "wo0": rows(a["L0_attn_Wo"].T), "gb": rows(np.stack([a["L0_attn_gamma"], a["L0_attn_beta"]], 1)),
        "wq1": rows(a["L1_attn_Wq"].T), "wk1": rows(a["L1_attn_Wk"].T), "wv1": rows(a["L1_attn_Wv"].T),
        "wo1": tiles(a["L1_attn_Wo"].T), "rw": rows(a["L1_ffn_router_w"].T),
        "rbias": rows(np.broadcast_to(a["L1_ffn_router_bias"], (P, NT, NE))),
        "sw1": rows(a["L1_ffn_sw1"]), "sw3": rows(a["L1_ffn_sw3"]), "sw2": tiles(a["L1_ffn_sw2"]),
        "ew1": rows(a["L1_ffn_ew1"].transpose(1, 0, 2)), "ew2": rows(a["L1_ffn_ew2"].transpose(1, 0, 2)),
    }
    p, q = np.arange(P)[:, None], np.arange(P)[None, :]
    j = np.arange(GH)[None, :]
    consts = {
        "ident": (p == q), "negmask": np.where(q > p, MASKED, 0.0),
        "headmask": np.where(p < OFF_ROW, (p % 32) // HD0 == j, p == OFF_ROW + j),
        "spread": (p // 32 == q // HD1) & (p % 32 < 3),
        "pairmask": (p % 32) // FEAT == np.arange(2)[None, :],
        "iota8": np.broadcast_to(np.arange(NE), (P, NT, NE)),
    }
    consts = {k: np.ascontiguousarray(v, dtype=np.float32) for k, v in consts.items()}

    nc = _bacc.Bacc("TRN2", target_bir_lowering=False, num_devices=1)
    arrays = {"x_dram": rows(a["L0_attn_x"])}

    def dram(name, array):
        arrays[name] = array
        return nc.dram_tensor(name, array.shape, mybir.dt.from_np(array.dtype), kind="ExternalInput").ap()

    x_ap = dram("x_dram", arrays["x_dram"])
    w_aps = {k: dram(f"{k}_dram", v) for k, v in weights.items()}
    c_aps = {k: dram(f"{k}_const", v) for k, v in consts.items()}
    out_ap = nc.dram_tensor("out_dram", (B, S, D), F32, kind="ExternalOutput").ap()
    build_program(nc, x_ap, w_aps, c_aps, out_ap)
    r = _run(nc, [arrays], core_ids=[0])
    return r.results[0]["out_dram"]
```

```python
from contextlib import ExitStack

import numpy as np

import concourse.bass as bass
from concourse import mybir

F32 = mybir.dt.float32
F16 = mybir.dt.float16
BF16 = mybir.dt.bfloat16
U32 = mybir.dt.uint32
ALU = mybir.AluOpType
ACT = mybir.ActivationFunctionType
AX = mybir.AxisListType

B, S, D = 8, 512, 128
P = 128
NT = S // P
LN_EPS = 1e-5
F0, R0 = 512, 32
NF = F0 // P
H0, HD0 = 16, 8
GH = 4
NG = H0 // GH
VC = 32
OFF_ROW = 96
OFF_UNIT = 64.0
H1, FEAT, HD1 = 16, 16, 64
NPAIR = H1 // 2
TAYLOR_EPS = 1e-12
HS, HR, NE = 256, 128, 8
NS = HS // P
GATE_EPS = 1e-9
MASKED = -1e30
W_SCALE = 64.0
PAIR_COLS = {"sw1": HS, "sw3": HS, "ew1": NE * HR, "wq1": H1 * FEAT, "wk1": H1 * FEAT, "wv1": H1 * HD1, "rw": NE}

WIDTH = [S - P * kt for kt in range(NT)]


def segment(kt, head, heads):
    if kt == 0:
        return head * S
    if kt == 1:
        return (heads + head) * S
    if kt == 3:
        return (heads + head) * S + WIDTH[1]
    return 2 * heads * S + head * WIDTH[2]


def units_of(heads):
    return ([[(0, h)] for h in range(heads)] + [[(1, h), (3, h)] for h in range(heads)]
            + [[(2, h), (2, h + 1)] for h in range(0, heads, 2)])


UNITS0, UNITS1 = units_of(GH), units_of(2)
COLS0, COLS1 = len(UNITS0) * S, len(UNITS1) * S

NU0, NU1 = len(UNITS0), len(UNITS1)
COMPLETE0 = {GH - 1: (0,), 2 * GH - 1: (1, 3), NU0 - 1: (2,)}
COMPLETE1 = {1: (0,), 3: (1, 3), 4: (2,)}
NC = len(COMPLETE1)
OUT1_PAIRS = (range(NPAIR - 2), range(NPAIR - 2, NPAIR))

def listed(text):
    out = []
    for word in text.split():
        name, _, numbers = word.partition(".")
        first, _, last = numbers.partition("-")
        out += [f"{name} {n}" for n in range(int(first), int(last or first) + 1)] if numbers else [name]
    return out


ORDER_A = listed("""
    load stat.0 centre.0 norm.0 up0.0-1 down0.0-1 stat.1 centre.1 norm.1 qkv0 pad0.0 max.0-3 pad0.1 max.4-10
    pad0.2 max.11-19 shift.0 max.20-22 shift.1 max.23-25 pad0.3 max.26-27 exp.0 max.28 exp.1-5 max.29
    exp.6-7 max.30 exp.8-12 max.31-32 shift.2 max.33-34 exp.13-14 max.35-36 pv0.0 exp.15 max.37 exp.16
    max.38 exp.17 max.39 exp.18-20 shift.3 turn.0 exp.21-26 pv0.1 exp.27-37 pv0.2 turn.1 exp.38-39 pv0.3
    turn.2-3 stat.2 centre.2 norm.2 out0 stat.3 centre.3 norm.3 up0.2-3 down0.2-3""")
ORDER_B = listed("""
    take stat.0 centre.0 split.0 router.0 gate.0-1 route.0 expert.0-7 stat.1 centre.1 split.1 qk1 v1.0-1
    pad1.0 v1.2-3 pad1.1-3 sq.0-7 den.0 sq.8-9 num.0 sq.10-11 scale.0 den.1 sq.12-14 num.1 sq.15-17 scale.1
    den.2 sq.18-19 num.2 sq.20-22 scale.2 den.3 sq.23-24 num.3 sq.25-27 scale.3 den.4 sq.28-29 num.4 sq.30
    scale.4 sq.31 den.5 sq.32-34 num.5 scale.5 sq.35 den.6 sq.36-39 num.6 scale.6 den.7 num.7 scale.7
    out1.0-1 stat.2 centre.2 split.2 router.1 gate.2-3 route.1 expert.8-15 store""")
LOOP = "".join("""
    BBABABABBABBAAAAABABBABABBBBBABAAABAAABAAAAABAABAAABABAABBABAAABAABABBAABABAABABBBABABBBABAABBBAAABB
    BBABAABABBABABAABAABABAABABBBAAABBABBABAABBAABBABBBAAABBBBAAABBBAABABBAAABAAABBABBBAAABAABABBAABAAAA
    BABAABABABABBABABBABBABABAABA""".split())


def ring_uses(step):
    name, _, n = step.partition(" ")
    n = int(n or 0)
    if name == "norm":
        return [("lnT", "act")]
    if name == "split":
        return [("lnT", "dve")]
    if name == "up0":
        return [(f"up{f}", "act") for f in ((0, 1), (2, 3))[n % 2]]
    if name == "down0" and n % 2 == 0:
        return []
    if name in ("down0", "out0", "out1"):
        return [("y", "dve")]
    if name == "qkv0":
        return [("q", "dve"), ("k", "dve"), ("v", "act")]
    if name == "max":
        return [("s", "dve")]
    if name == "shift":
        return [("mT", "act")]
    if name in ("exp", "sq"):
        return [("s", "act")]
    if name == "turn":
        return [("o", "dve")]
    if name == "router":
        return [("router", "act")]
    if name == "gate":
        return [("gate", "dve"), ("lin", "dve")]
    if name == "expert":
        e = n % NE
        return [(f"e{k}", "act") for k in ([0, 1] if e == 0 else [e + 1] if e + 1 < NE else [])]
    if name == "qk1":
        return [(f"{x}{t}", "dve") for x in "qk" for t in range(2)]
    if name == "v1":
        return [("low", "act"), ("high", "dve")]
    if name == "scale":
        return [("r", "dve")]
    return []


def unit_of_expert(n, e):
    return f"expert {NE * n + max(e - 1, 0)}", f"e{e}"


def ring_table(order, banks):
    table, drained = {}, {"act": 0, "dve": 0}
    listed = [(step, u, e) for step in order for u, e in ring_uses(step)]
    for n, (step, u, e) in enumerate(listed):
        drained[e] += 1
        before = table[listed[n - banks][:2]] if n >= banks else None
        table[step, u] = Unit(n + 1, n % banks, e, drained[e], before)
    return table, Totals(len(listed), drained["act"], drained["dve"])


def weave(a, b):
    rest = {"A": iter(a), "B": iter(b)}
    assert LOOP.count("A") == len(a) and LOOP.count("B") == len(b)
    return [(h, next(rest[h])) for h in LOOP]


class Unit:

    def __init__(self, n, bank, engine, count, before):
        self.n, self.bank, self.engine, self.count, self.before = n, bank, engine, count, before


class Totals:

    def __init__(self, filled, act, dve):
        self.filled, self.act, self.dve = filled, act, dve


class Half:
    pass


def bcast(ap, n):
    return bass.AP(ap.tensor, ap.offset, [list(x) for x in ap.ap[:-1]] + [[0, n]])


class Chain:

    def __init__(self, eng, sem, per):
        self.eng, self.sem, self.per, self.n, self.it = eng, sem, per, 0, 0

    def start(self, it):
        self.it, self.n = it, 0

    def then(self, ins, carrier=None):
        self.n += 1
        ins.then_inc(self.sem, 1)
        self.eng.wait_ge(self.sem, self.it * self.per + self.n)
        if carrier is not None:
            carrier()

    def end(self):
        assert self.n == self.per, (self.n, self.per)


def build_program(nc, x, w, cst, out):
    ctx = ExitStack()
    with ctx:
        def sb(name, shape, dt=F32):
            return ctx.enter_context(nc.sbuf_tensor(name, shape, dt))

        def sem(name):
            return ctx.enter_context(nc.semaphore(name))

        banks = [ctx.enter_context(nc.psum_tensor(f"bank{i}", [P, S], F32)) for i in range(8)]
        ringA, accA = banks[0:3], banks[3]
        ringB, numB, denB = banks[4:6], banks[6], banks[7]
        TA, PERA = ring_table(ORDER_A, len(ringA))
        TB, PERB = ring_table(ORDER_B, len(ringB))

        ident = sb("ident", [P, P])
        identb = sb("identb", [P, P], BF16)
        negmask = sb("negmask", [P, P], BF16)
        headmask = sb("headmask", [P, GH])
        pairmask = sb("pairmask", [P, 2])
        iota8 = sb("iota8", [P, NT, NE])
        ones = sb("ones", [P, 32])
        spread = sb("spread", [P, P], BF16)
        neghalf = sb("neghalf", [P, NT])
        epsilon = sb("epsilon", [P, NT])
        spare_dve = sb("spare_dve", [1, 1])
        w1 = sb("w1", [P, F0])
        w2 = sb("w2", [P, NF, D])
        b1 = sb("b1", [P, NF]); b2h = sb("b2h", [P, NT, D])
        wq0 = sb("wq0", [P, D]); wk0 = sb("wk0", [P, D]); wv0 = sb("wv0", [P, D]); wo0 = sb("wo0", [P, D])
        gb = sb("gb", [P, 2])
        pairs = sb("pairs", [P, 2, sum(PAIR_COLS.values())], F16)
        wo1 = sb("wo1", [P, NPAIR, D])
        rbias = sb("rbias", [P, NT, NE])
        sw2 = sb("sw2", [P, NS, D])
        ew2 = sb("ew2", [P, NE, D])

        def half(name):
            h = Half()
            h.x = sb(f"x{name}", [P, NT, D])
            h.ln = sb(f"ln{name}", [P, NT, D])
            if name == "A":
                h.lnT = sb("lnTA", [P, S])
            else:
                h.lnT_hi, h.lnT_lo = sb("lnTB_hi", [P, S], F16), sb("lnTB_lo", [P, S], F16)
            h.stats, h.mv = sb(f"stats{name}", [P, NT, 6]), sb(f"mv{name}", [P, NT, 2])
            h.vare, h.rstd = sb(f"vare{name}", [P, NT]), sb(f"rstd{name}", [P, NT])
            h.spare = sb(f"spare{name}", [1, 1])
            h.filled = sem(f"filled{name}")
            h.act, h.dve = sem(f"drained_act{name}"), sem(f"drained_dve{name}")
            h.x_ready = sem(f"x_ready{name}")
            h.mv_ready, h.vare_ready = sem(f"mv_ready{name}"), sem(f"vare_ready{name}")
            h.rstd_ready, h.ln_ready = sem(f"rstd_ready{name}"), sem(f"ln_ready{name}")
            h.hi_ready = sem(f"hi_ready{name}")
            h.dve_step = sem(f"dve_step{name}")
            h.carried = sem(f"carried{name}")
            return h

        A, Bh = half("A"), half("B")
        A.ring, Bh.ring, A.T, Bh.T, A.per, Bh.per = ringA, ringB, TA, TB, PERA, PERB
        A.lns, Bh.lns = 4, 3
        A.carriers, Bh.carriers = NC * NG, NC * NPAIR
        A.name, Bh.name = "A", "B"
        probs = sb("probs", [P, 2, COLS0])
        hid0 = probs[:, 1, 0:NF * S].rearrange("p (f s) -> p f s", f=NF)
        p16 = probs[:, 0, :].bitcast(F16)
        q0h, q0l, k0h, k0l = (p16[:, i * S:(i + 1) * S] for i in range(4))
        kall = p16[:, 4 * S:(4 + NG) * S].rearrange("p (g s) -> p g s", g=NG)
        q0a = sb("q0a", [P, NG, S], F16)
        kpad0 = sb("kpad0", [P, H0, S], F16)
        vaug = sb("vaug", [P, NT, H0, HD0 + 1])
        bmax = sb("bmax", [P, len(UNITS0) * NT])
        rmax = sb("rmax", [P, NT, H0])
        offs = sb("offs", [GH, NG, S], F16)
        oT = sb("oT", [P, 2, S])
        rden = sb("rden", [P, NG, NT, GH, 1])
        attn = sb("attn", [P, NT, D])
        mid = sb("mid", [P, NT, D])
        yT = sb("yT", [P, NPAIR, S])
        wts = sb("wts", [P, 2, COLS1])
        sgm, hsh, hexp = yT[:, 0:NS, :], yT[:, NS:2 * NS, :], yT[:, 2 * NS:2 * NS + 2, :]
        k1a = yT[0:96, 0:NPAIR // 2, :].rearrange("p a s -> p (a s)").bitcast(F16)\
            .rearrange("p (a s) -> p a s", s=S)
        w16 = wts[:, 0, :].bitcast(F16)
        q1h, q1l, k1h, k1l = (w16[:, 2 * i * S:2 * (i + 1) * S].rearrange("p (t s) -> p t s", t=2)
                              for i in range(4))
        unsplit = yT[:, :, :].rearrange("p a s -> p (a s)")
        first_col, n = {}, 0
        for name, cols in PAIR_COLS.items():
            first_col[name], n = n, n + cols

        def staged(name):
            return unsplit[:, first_col[name]:first_col[name] + PAIR_COLS[name]]

        U1T, V1 = wts[0:R0, 0, 0:D], wts[0:R0, 0, D:D + F0]
        U2T, V2 = wts[0:R0, 1, 0:F0], wts[0:R0, 1, F0:F0 + D]
        negf = wts[:, 1, F0 + D:F0 + D + P]
        spreadf = wts[:, 1, F0 + D + P:F0 + D + 2 * P]
        s8 = sb("s8", [P, NT, NE]); sel = sb("sel", [P, NT, NE]); top = sb("top", [P, NT, 8])
        idx = sb("idx", [P, NT, 8], U32); idf = sb("idf", [P, NT, 2])
        oh = sb("oh", [P, 2, NT, NE]); pick = sb("pick", [P, NT, NE]); ssel = sb("ssel", [P, NT, NE])
        den = sb("den", [P, NT, 1]); dsafe = sb("dsafe", [P, NT, 1]); half_if = sb("half_if", [P, NT, 1])
        rdn = sb("rdn", [P, NT, 1]); rsc = sb("rsc", [P, NT, 1]); flat = sb("flat", [P, NT, 1])
        gsc = sb("gsc", [P, NT, NE]); gfl = sb("gfl", [P, NT, NE]); comb = sb("comb", [P, NT, NE])
        acc = Bh.ln
        q1a = sb("q1a", [96, NPAIR, S], F16)
        kpad1 = sb("kpad1", [96, H1, S], F16)
        v1 = sb("v1", [P, NT, H1 * HD1])
        d32 = sb("d32", [P, S])
        dlate = sb("dlate", [HD1, S // 32]); dsum = sb("dsum", [HD1, S // 32]); rrec = sb("rrec", [HD1, S // 32])
        rrem = sb("rrem", [HD1, S // 32])
        rsplit = sb("rsplit", [P, S], BF16)
        rrows = sb("rrows", [P, S], BF16)
        res = sb("res", [P, NT, D])

        w_first = sem("w_first"); w_rest = sem("w_rest"); hi_split = sem("hi_split"); w_split = sem("w_split")
        lnT_hi_ready = sem("lnT_hi_ready"); setup = sem("setup"); tables = sem("tables")
        b2_halved = sem("b2_halved")
        lowrank = sem("lowrank"); lowrank_copied = sem("lowrank_copied")
        qk0_laid = [sem(f"qk0_laid{g}") for g in range(NG)]
        qk1_laid = [sem(f"qk1_laid{n}") for n in range(4)]
        kpad0_ready = sem("kpad0_ready"); kpad1_ready = sem("kpad1_ready")
        rmax_ready = sem("rmax_ready"); offs_ready = sem("offs_ready")
        offs_laid = [sem(f"offs_laid{g}") for g in range(NG)]
        masked0 = sem("masked0"); pv0_done = sem("pv0_done"); oT_ready = sem("oT_ready")
        mid_taken = sem("mid_taken")
        gate_ready = sem("gate_ready"); hsh_ready = sem("hsh_ready")
        moe_out = sem("moe_out"); moe_added = sem("moe_added")
        plus1 = sem("plus1"); masked1 = sem("masked1"); pv1_done = sem("pv1_done")
        den_done = sem("den_done"); den_read = sem("den_read"); num_read = sem("num_read")
        rrows_ready = sem("rrows_ready")
        res_free = sem("res_free")

        NW = len(w) + len(cst)
        SETUP = 8
        NW_FIRST = 11
        DVE_A, DVE_B = 10, 85
        QK_DMAS = 6
        order_loop = weave(ORDER_A, ORDER_B)

        def steps(fns, it_of, order):
            for h, step in order:
                name, _, n = step.partition(" ")
                if name in ("stat", "centre", "norm") and name in fns:
                    fns[name](A if h == "A" else Bh, it_of[h], int(n), step)
                elif name in fns:
                    fns[name](it_of[h], int(n or 0), step)

        def run(eng, fns, start=None, end=None):
            def part(it_of, order):
                if start:
                    start(it_of)
                steps(fns, it_of, order)
                if end:
                    end(it_of)
            part({"A": 0}, [("A", s) for s in ORDER_A])
            with eng.Fori(0, B - 1) as i:
                part({"A": i + 1, "B": i}, order_loop)
            part({"B": B - 1}, [("B", s) for s in ORDER_B])

        def fill(pe, h, it, step, unit):
            u = h.T[step, unit]
            if u.before:
                s = {"act": h.act, "dve": h.dve}[u.before.engine]
                pe.wait_ge(s, it * (h.per.act if u.before.engine == "act" else h.per.dve) + u.before.count)
            return h.ring[u.bank]

        def full(eng, h, it, step, unit):
            u = h.T[step, unit]
            eng.wait_ge(h.filled, it * h.per.filled + u.n)
            return h.ring[u.bank]

        def drained(h, it, step, unit):
            u = h.T[step, unit]
            return it * (h.per.act if u.engine == "act" else h.per.dve) + u.count

        block = ctx.enter_context(nc.Block())

        @block.sync
        def _(sp):
            def load(it, _n, step):
                if not isinstance(it, int):
                    sp.wait_ge(A.dve, drained(A, it, "down0 3", "y") - A.per.dve)
                sp.dma_start(A.x[:, :, :], x[bass.ds(it, 1), :, :].rearrange("a (t p) d -> p (a t) d", p=P))\
                  .then_inc(A.x_ready, 16)

            load(0, 0, "load")
            tiles = dict(ident=ident[:], headmask=headmask[:], U1T=U1T, V1=V1, U2T=U2T, V2=V2, b1=b1[:], b2=b2h[:],
                         negmask=negf, spread=spreadf, pairmask=pairmask[:], iota8=iota8[:], wq0=wq0[:], wk0=wk0[:],
                         wv0=wv0[:], wo0=wo0[:], gb=gb[:], wo1=wo1[:], rbias=rbias[:], sw2=sw2[:],
                         ew2=ew2[:], **{name: staged(name) for name in PAIR_COLS})
            source = {**w, **cst}
            assert list(tiles)[:NW_FIRST][-1] == "pairmask" and set(tiles) == set(source)
            for n, name in enumerate(tiles):
                sp.dma_start(tiles[name], source[name]).then_inc(w_first if n < NW_FIRST else w_rest, 16)

            def qkv0(it, _n, step):
                sp.wait_ge(A.dve, drained(A, it, step, "k"))
                for g in range(NG):
                    rows = slice(32 * g, 32 * g + 32)
                    for dst, parts in ((q0a, (q0h, q0h, q0l)), (kall, (k0h, k0l, k0h))):
                        for a, part in enumerate(parts):
                            sp.dma_start(dst[32 * a:32 * a + 32, g, :], part[rows, :]).then_inc(qk0_laid[g], 16)

            def shift(it, g, step):
                sp.wait_ge(A.act, drained(A, it, step, "mT"))
                sp.dma_start(q0a[OFF_ROW:OFF_ROW + GH, g, :], offs[:, g, :]).then_inc(offs_laid[g], 16)

            def qk1(it, _n, step):
                sp.wait_ge(Bh.dve, drained(Bh, it, step, "k1"))
                for n in range(4):
                    rows = slice(32 * n, 32 * n + 32)
                    for dst, parts in ((q1a, (q1h, q1h, q1l)), (k1a, (k1h, k1l, k1h))):
                        for a, part in enumerate(parts):
                            sp.dma_start(dst[32 * a:32 * a + 32, n:NPAIR:4, :], part[rows, :, :])\
                              .then_inc(qk1_laid[n], 16)

            def store(it, _n, step):
                sp.wait_ge(moe_added, (it * 2 + 2) * (NE + 1))
                sp.dma_start(out[bass.ds(it, 1), :, :].rearrange("a (t p) d -> p (a t) d", p=P), res[:, :, :])\
                  .then_inc(res_free, 16)

            def load_next(it, _n, step):
                if not isinstance(it, int):
                    load(it, _n, step)

            run(sp, dict(load=load_next, qkv0=qkv0, shift=shift, qk1=qk1, store=store))
            sp.wait_ge(res_free, 16 * (B + 1))

        @block.gpsimd
        def _(pool):
            pool.memset(vaug[:, :, :, HD0:HD0 + 1], 1.0).then_inc(setup, 1)
            pool.memset(neghalf[:, :], -0.5).then_inc(setup, 1)
            pool.memset(epsilon[:, :], LN_EPS).then_inc(setup, 1)
            pool.memset(ones[:, :], 1.0).then_inc(setup, 1)
            pool.wait_ge(setup, SETUP)
            for h in (A, Bh):
                pool.tensor_tensor(h.spare[:, :], neghalf[0:1, 0:1], neghalf[0:1, 0:1], ALU.add).then_inc(h.carried, 1)

            def ln_scale(h, it, k, step):
                pool.wait_ge(h.mv_ready, it * h.lns + k + 1)
                pool.tensor_tensor(h.vare[:, :], h.mv[:, :, 1], epsilon[:, :], ALU.add).then_inc(h.vare_ready, 1)
                pool.wait_ge(h.vare_ready, it * h.lns + k + 1)
                pool.tensor_tensor(h.rstd[:, :], h.vare[:, :], neghalf[:, :], ALU.pow).then_inc(h.rstd_ready, 1)

            def wait_apart(h, it, n, sem, value):
                pool.wait_ge(h.carried, it * h.carriers + n + 1)
                pool.wait_ge(sem, value)
                pool.tensor_tensor(h.spare[:, :], neghalf[0:1, 0:1], neghalf[0:1, 0:1], ALU.add).then_inc(h.carried, 1)

            def mask(buf, heads, kt):
                step = {0: S, 1: S, 3: S, 2: WIDTH[2]}[kt]
                s0 = segment(kt, 0, heads)
                v = bass.AP(buf.tensor, buf.offset + s0, [list(buf.ap[0]), [step, heads], [1, P]])
                return pool.affine_select(out=v, in_=v, compare_op=ALU.is_ge, fill=0.0, base=0,
                                          pattern=[[0, heads], [1, P]], channel_multiplier=-1)

            def exp(it, n, step):
                g, u = divmod(n, NU0)
                if u in COMPLETE0:
                    wait_apart(A, it, g * NC + list(COMPLETE0).index(u), A.act, drained(A, it, step, "s"))
                for kt in COMPLETE0.get(u, ()):
                    mask(probs[:, g % 2, :], GH, kt).then_inc(masked0, 1)

            def sq(it, n, step):
                p, u = divmod(n, NU1)
                if u in COMPLETE1:
                    k = p * NC + list(COMPLETE1).index(u)
                    wait_apart(Bh, it, k, plus1, it * NPAIR * NC + k + 1)
                for kt in COMPLETE1.get(u, ()):
                    mask(wts[:, p % 2, :], 2, kt).then_inc(masked1, 1)

            run(pool, dict(stat=ln_scale, exp=exp, sq=sq))

        @block.scalar
        def _(act):
            act.wait_ge(w_first, 16 * NW_FIRST)
            act.wait_ge(setup, SETUP)
            for j in range(GH):
                act.activation(kpad0[OFF_ROW:P, j:H0:GH, :], q0a[OFF_ROW:P, :, :], ACT.Identity,
                               bias=headmask[OFF_ROW:P, j:j + 1]).then_inc(tables, 1)
            act.wait_ge(lowrank, 1)
            act.activation(w1[:, :], ringA[0][:, :], ACT.Copy).then_inc(lowrank_copied, 1)
            act.activation(w2[:, :, :].rearrange("p a b -> p (a b)"), ringA[1][:, :], ACT.Copy)\
               .then_inc(lowrank_copied, 1)
            act.activation(identb[:, :], ident[:, :], ACT.Copy).then_inc(tables, 1)
            act.activation(negmask[:, :], negf[:, :], ACT.Copy).then_inc(tables, 1)
            act.activation(spread[:, :], spreadf[:, :], ACT.Copy).then_inc(tables, 1)

            def norm(h, it, k, step):
                ps = full(act, h, it, step, "lnT")
                if h is A and k == 2:
                    act.activation(h.lnT[:, :], ps[:, :], ACT.Identity, bias=gb[:, 1:2], scale=gb[:, 0:1])\
                       .then_inc(h.act, 1)
                else:
                    act.activation(h.lnT[:, :], ps[:, :], ACT.Copy).then_inc(h.act, 1)

            def split(it, k, step):
                ps = full(act, Bh, it, step, "lnT")
                act.activation(Bh.lnT_hi[:, :], ps[:, :], ACT.Copy).then_inc(lnT_hi_ready, 1)

            def up0(it, n, step):
                for unit, _ in ring_uses(step):
                    f = int(unit[2:])
                    ps = full(act, A, it, step, unit)
                    act.activation(hid0[:, f, :], ps[:, :], ACT.Gelu_apprx_tanh, bias=b1[:, f:f + 1])\
                       .then_inc(A.act, 1)

            def qkv0(it, n, step):
                ps = full(act, A, it, step, "q")
                act.activation(q0h[:, :], ps[:, :], ACT.Copy).then_inc(A.hi_ready, 1)
                ps = full(act, A, it, step, "k")
                act.activation(k0h[:, :], ps[:, :], ACT.Copy, scale=HD0 ** -0.5).then_inc(A.hi_ready, 1)
                ps = full(act, A, it, step, "v")
                act.wait_ge(setup, SETUP)
                act.activation(vaug[:, :, :, 0:HD0].rearrange("p t h d -> p (t h) d"),
                               ps[:, :].rearrange("p (a d) -> p a d", d=HD0), ACT.Copy).then_inc(A.act, 1)

            def shift(it, g, step):
                ps = full(act, A, it, step, "mT")
                act.activation(offs[:, g, :], ps[0:GH, :], ACT.Copy, scale=-1.0 / OFF_UNIT).then_inc(A.act, 1)

            def exp(it, n, step):
                g, u = divmod(n, NU0)
                if n == 0:
                    act.wait_ge(kpad0_ready, it * NG + NG)
                if g >= 2 and u == 0:
                    act.wait_ge(pv0_done, it * NG + g - 1)
                ps = full(act, A, it, step, "s")
                act.activation(probs[:, g % 2, u * S:(u + 1) * S], ps[:, :], ACT.Exp).then_inc(A.act, 1)

            def router(it, n, step):
                ps = full(act, Bh, it, step, "router")
                act.activation(s8[:, :, :].rearrange("p t e -> p (t e)"), ps[:, 0:NT * NE], ACT.Sigmoid,
                               scale=1 / W_SCALE)\
                   .then_inc(Bh.act, 1)

            def gate(it, n, step):
                ps = full(act, Bh, it, step, "gate")
                act.activation(sgm[:, n % NS, :], ps[:, :], ACT.Sigmoid, scale=1 / W_SCALE)\
                   .then_inc(gate_ready, 1)

            def expert(it, n, step):
                for unit, _ in ring_uses(step):
                    e = int(unit[1:])
                    ps = full(act, Bh, it, step, unit)
                    if e >= 2:
                        act.wait_ge(moe_out, (it * 2 + n // NE) * (NE + 1) + 1 + e - 1)
                    act.activation(hexp[:, e % 2, :], ps[:, :], ACT.Gelu, scale=1 / W_SCALE)\
                       .then_inc(Bh.act, 1)

            def qk1(it, n, step):
                for name, hi in (("q", q1h), ("k", k1h)):
                    for t in range(2):
                        ps = full(act, Bh, it, step, f"{name}{t}")
                        act.activation(hi[:, t, :], ps[:, :], ACT.Copy, scale=1 / W_SCALE).then_inc(Bh.hi_ready, 1)

            def values1(it, t, step):
                ps = full(act, Bh, it, step, "low")
                act.activation(v1[:, t, 0:S], ps[:, :], ACT.Copy).then_inc(Bh.act, 1)

            def sq(it, n, step):
                p, u = divmod(n, NU1)
                if n == 0:
                    act.wait_ge(kpad1_ready, it * 4 + 4)
                if p >= 2 and u == 0:
                    act.wait_ge(pv1_done, it * NPAIR + p - 1)
                ps = full(act, Bh, it, step, "s")
                act.activation(wts[:, p % 2, u * S:(u + 1) * S], ps[:, :], ACT.Square,
                               bias=1.0, scale=FEAT ** -0.5).then_inc(Bh.act, 1)

            def num(it, p, step):
                act.wait_ge(pv1_done, it * NPAIR + p + 1)
                act.activation(yT[:, p, :], numB[:, :], ACT.Copy).then_inc(num_read, 1)

            fns = dict(norm=norm, split=split, up0=up0, qkv0=qkv0, shift=shift, exp=exp, router=router, gate=gate,
                       expert=expert, qk1=qk1, v1=values1, sq=sq, num=num)
            run(act, fns)

        @block.vector
        def _(dve):
            def carrier():
                dve.memset(spare_dve[:, :], 0.0)

            chA, chB = Chain(dve, A.dve_step, DVE_A), Chain(dve, Bh.dve_step, DVE_B)
            dve.memset(q0a[OFF_ROW:P, :, :], 0.0).then_inc(setup, 1)
            dve.memset(accA[:, :], 0.0).then_inc(setup, 1)
            dve.memset(rsplit[:, :], 0.0).then_inc(setup, 1)
            dve.memset(dlate[:, :], 0.0).then_inc(setup, 1)
            dve.memset(res[:, :, :], 0.0).then_inc(res_free, 16)
            dve.wait_ge(w_first, 16 * NW_FIRST)
            dve.tensor_scalar(b2h[:, :, :], b2h[:, :, :], 0.5, None, ALU.mult).then_inc(b2_halved, 1)
            dve.wait_ge(b2_halved, 1)
            dve.wait_ge(setup, SETUP)

            def stat(h, it, k, step):
                ch, src = (chA, attn if k == 2 else A.x) if h is A else (chB, Bh.x)
                if h is A and k == 0:
                    dve.wait_ge(A.x_ready, (it + 1) * 16)
                elif h is A:
                    before = {1: ("down0 1", "y"), 2: (f"turn {NG - 1}", "o"), 3: ("out0", "y")}[k]
                    dve.wait_ge(A.dve, drained(A, it, *before))
                elif k == 0:
                    dve.wait_ge(mid_taken, it + 1)
                elif k == 1:
                    dve.wait_ge(moe_added, (it * 2 + 1) * (NE + 1))
                else:
                    dve.wait_ge(Bh.dve, drained(Bh, it, "out1 1", "y"))
                for t in range(NT):
                    last = dve.bn_stats(h.stats[:, t, :], src[:, t, :])
                ch.then(last, carrier)
                for t in range(NT):
                    last = dve.bn_aggr(h.mv[:, t, :], h.stats[:, t, :])
                last.then_inc(h.mv_ready, 1)

            def centre(h, it, k, step):
                src = Bh.x if h is Bh else attn if k == 2 else A.x
                dve.wait_ge(h.rstd_ready, it * h.lns + k + 1)
                for t in range(NT):
                    last = dve.tensor_scalar(h.ln[:, t, :], src[:, t, :], h.mv[:, t, 0:1], h.rstd[:, t:t + 1],
                                             ALU.subtract, ALU.mult)
                last.then_inc(h.ln_ready, 1)

            def down0(it, n, step):
                if n % 2 == 0:
                    full(dve, A, it, f"norm {(0, 3)[n // 2]}", "lnT")
                    chA.then(dve.tensor_tensor(A.ln[:, :, :], A.x[:, :, :], b2h[:, :, :], ALU.add))
                    return
                ps = full(dve, A, it, step, "y")
                dst = A.x if n == 1 else mid
                if n == 3 and not isinstance(it, int):
                    dve.wait_ge(mid_taken, it)
                dve.scalar_tensor_tensor(out=dst[:, :, :].rearrange("p t d -> p (t d)"), in0=ps[:, :],
                                         scalar=0.5, in1=A.ln[:, :, :].rearrange("p t d -> p (t d)"),
                                         op0=ALU.mult, op1=ALU.add).then_inc(A.dve, 1)

            def split(it, k, step):
                ps = full(dve, Bh, it, step, "lnT")
                dve.wait_ge(lnT_hi_ready, it * Bh.lns + k + 1)
                dve.tensor_tensor(Bh.lnT_lo[:, :], ps[:, :], Bh.lnT_hi[:, :], ALU.subtract).then_inc(Bh.dve, 1)

            def split_weights():
                w_in = unsplit[:, 0:sum(PAIR_COLS.values())]
                dve.wait_ge(w_rest, 16 * (NW - NW_FIRST))
                dve.tensor_scalar(pairs[:, 0, :], w_in, W_SCALE, None, ALU.mult).then_inc(hi_split, 1)
                dve.tensor_scalar(sw2[:, :, :], sw2[:, :, :], W_SCALE ** -2, None, ALU.mult)
                dve.tensor_scalar(wo1[:, :, :], wo1[:, :, :], 1 / W_SCALE, None, ALU.mult)
                dve.wait_ge(hi_split, 1)
                dve.scalar_tensor_tensor(out=pairs[:, 1, :], in0=w_in, scalar=W_SCALE, in1=pairs[:, 0, :],
                                         op0=ALU.mult, op1=ALU.subtract).then_inc(w_split, 1)

            def qkv0(it, n, step):
                for i, (name, hi, lo, sc) in enumerate((("q", q0h, q0l, 1.0), ("k", k0h, k0l, HD0 ** -0.5))):
                    ps = full(dve, A, it, step, name)
                    dve.wait_ge(A.hi_ready, it * 2 + i + 1)
                    dve.scalar_tensor_tensor(out=lo[:, :], in0=ps[:, :], scalar=sc, in1=hi[:, :],
                                             op0=ALU.mult, op1=ALU.subtract).then_inc(A.dve, 1)
                if isinstance(it, int):
                    split_weights()

            def pad0(it, g, step):
                dve.wait_ge(qk0_laid[g], (it + 1) * 16 * QK_DMAS)
                dve.memset(q0a[OFF_ROW:P, g, :], 0.0)
                for hd in range(GH * g, GH * g + GH):
                    last = dve.tensor_scalar(kpad0[0:OFF_ROW, hd, :], kall[0:OFF_ROW, g, :],
                                             headmask[0:OFF_ROW, hd % GH:hd % GH + 1], None, ALU.mult)
                last.then_inc(kpad0_ready, 1)

            def rowmax(it, n, step):
                g, u = divmod(n, NU0)
                ps = full(dve, A, it, step, "s")
                dve.tensor_reduce(bmax[:, u * NT:(u + 1) * NT], ps[:, :].rearrange("p (b k) -> p b k", k=P),
                                  AX.X, ALU.max).then_inc(A.dve, 1)
                if u < NU0 - 1:
                    return
                dve.wait_ge(A.dve, drained(A, it, step, "s"))
                heads = slice(g * GH, (g + 1) * GH)
                wide = bmax[:, 0:GH * NT].rearrange("p (h b) -> p h b", b=NT)
                pair = bmax[:, GH * NT:2 * GH * NT].rearrange("p (h b) -> p h b", b=NT)
                two = bmax[:, 2 * GH * NT:].rearrange("p (h b) -> p h b", b=2)
                dve.tensor_reduce(rmax[:, 3, heads], wide, AX.X, ALU.max)
                dve.tensor_reduce(rmax[:, 2, heads], pair[:, :, 0:3], AX.X, ALU.max)
                dve.tensor_reduce(rmax[:, 1, heads], two, AX.X, ALU.max)
                dve.tensor_reduce(rmax[:, 0, heads], pair[:, :, 3:4], AX.X, ALU.max).then_inc(rmax_ready, 1)
                dve.wait_ge(rmax_ready, it * NG + g + 1)

            def pv0(it, g, step):
                dve.wait_ge(pv0_done, it * NG + g + 1)
                dve.tensor_copy(oT[:, g % 2, :], accA[:, :]).then_inc(oT_ready, 1)

            def turn(it, g, step):
                ps = full(dve, A, it, step, "o")
                v = ps[:, :].rearrange("p (t h c) -> p t h c", t=NT, c=VC)
                chA.then(dve.reciprocal(rden[:, g, :, :, :], v[:, :, :, HD0:HD0 + 1]))
                dst = attn[:, :, g * GH * HD0:(g + 1) * GH * HD0].rearrange("p t (h c) -> p t h c", c=HD0)
                dve.tensor_tensor(dst, v[:, :, :, 0:HD0], bcast(rden[:, g, :, :, :], HD0), ALU.mult)\
                   .then_inc(A.dve, 1)

            def out0(it, n, step):
                ps = full(dve, A, it, step, "y")
                dve.tensor_tensor(A.x[:, :, :].rearrange("p t d -> p (t d)"), ps[:, :],
                                  A.x[:, :, :].rearrange("p t d -> p (t d)"), ALU.add).then_inc(A.dve, 1)

            def take(it, n, step):
                dve.wait_ge(A.dve, drained(A, it, "down0 3", "y"))
                dve.tensor_copy(Bh.x[:, :, :], mid[:, :, :]).then_inc(mid_taken, 1)

            def route(it, n, step):
                c = chB
                dve.wait_ge(Bh.act, drained(Bh, it, f"router {n}", "router"))
                c.then(dve.tensor_tensor(sel[:, :, :], s8[:, :, :], rbias[:, :, :], ALU.add), carrier)
                for t in range(NT):
                    last = dve.max(top[:, t, :], sel[:, t, :])
                c.then(last, carrier)
                for t in range(NT):
                    last = dve.max_index(idx[:, t, :], top[:, t, :], sel[:, t, :])
                c.then(last)
                c.then(dve.tensor_copy(idf[:, :, :], idx[:, :, 0:2]))
                for j in range(2):
                    last = dve.tensor_tensor(oh[:, j, :, :], iota8[:, :, :], bcast(idf[:, :, j:j + 1], NE),
                                             ALU.is_equal)
                c.then(last)
                c.then(dve.tensor_tensor(pick[:, :, :], oh[:, 0, :, :], oh[:, 1, :, :], ALU.add))
                c.then(dve.tensor_tensor(ssel[:, :, :], s8[:, :, :], pick[:, :, :], ALU.mult))
                c.then(dve.tensor_reduce(den[:, :, :], ssel[:, :, :], AX.X, ALU.add))
                dve.tensor_scalar(dsafe[:, :, :], den[:, :, :], GATE_EPS, None, ALU.add)
                c.then(dve.tensor_scalar(half_if[:, :, :], den[:, :, :], GATE_EPS, 0.5, ALU.is_gt, ALU.mult))
                c.then(dve.reciprocal(rdn[:, :, :], dsafe[:, :, :]))
                dve.tensor_scalar(flat[:, :, :], half_if[:, :, :], -0.5, 0.25, ALU.mult, ALU.add)
                c.then(dve.tensor_tensor(rsc[:, :, :], rdn[:, :, :], half_if[:, :, :], ALU.mult))
                dve.tensor_tensor(gsc[:, :, :], ssel[:, :, :], bcast(rsc[:, :, :], NE), ALU.mult)
                c.then(dve.tensor_tensor(gfl[:, :, :], pick[:, :, :], bcast(flat[:, :, :], NE), ALU.mult))
                c.then(dve.tensor_tensor(comb[:, :, :], gsc[:, :, :], gfl[:, :, :], ALU.add))

            def gate(it, nf, step):
                f = nf % NS
                ps = full(dve, Bh, it, step, "gate")
                dve.wait_ge(gate_ready, it * 2 * NS + nf + 1)
                dve.tensor_tensor(sgm[:, f, :], ps[:, :], sgm[:, f, :], ALU.mult).then_inc(Bh.dve, 1)
                dve.wait_ge(Bh.dve, drained(Bh, it, step, "gate"))
                ps = full(dve, Bh, it, step, "lin")
                dve.tensor_tensor(hsh[:, f, :], ps[:, :], sgm[:, f, :], ALU.mult).then_inc(Bh.dve, 1)

            def expert(it, ne, step):
                n, e = ne // NE, ne % NE
                first = (it * 2 + n) * (NE + 1)
                if e == 0:
                    dve.wait_ge(moe_out, first + 1)
                    dve.scalar_tensor_tensor(out=acc[:, :, :].rearrange("p t d -> p (t d)"), in0=numB[:, :],
                                             scalar=0.5, in1=Bh.x[:, :, :].rearrange("p t d -> p (t d)"),
                                             op0=ALU.mult, op1=ALU.add).then_inc(moe_added, 1)
                dve.wait_ge(moe_out, first + 2 + e)
                dve.wait_ge(moe_added, first + 1 + e)
                ps, dst = (denB, numB)[e % 2], acc
                if e == NE - 1:
                    dst = (Bh.x, res)[n]
                    if n == 1:
                        dve.wait_ge(res_free, 16 * (it + 1))
                for t in range(NT):
                    last = dve.scalar_tensor_tensor(out=dst[:, t, :], in0=ps[:, t * P:(t + 1) * P],
                                                    scalar=comb[:, t, e:e + 1], in1=acc[:, t, :],
                                                    op0=ALU.mult, op1=ALU.add)
                last.then_inc(moe_added, 1)

            def qk1(it, n, step):
                for i, (name, t, hi, lo) in enumerate((("q", 0, q1h, q1l), ("q", 1, q1h, q1l),
                                                       ("k", 0, k1h, k1l), ("k", 1, k1h, k1l))):
                    ps = full(dve, Bh, it, step, f"{name}{t}")
                    dve.wait_ge(Bh.hi_ready, it * 4 + i + 1)
                    dve.scalar_tensor_tensor(out=lo[:, t, :], in0=ps[:, :], scalar=1 / W_SCALE, in1=hi[:, t, :],
                                             op0=ALU.mult, op1=ALU.subtract).then_inc(Bh.dve, 1)

            def values1(it, t, step):
                ps = full(dve, Bh, it, step, "high")
                dve.tensor_copy(v1[:, t, S:2 * S], ps[:, :]).then_inc(Bh.dve, 1)

            def pad1(it, n, step):
                dve.wait_ge(qk1_laid[n], (it + 1) * 16 * QK_DMAS)
                for hd in (2 * n, 2 * n + 1, 2 * n + 8, 2 * n + 9):
                    last = dve.tensor_scalar(kpad1[:, hd, :], k1a[:, hd // 2, :], pairmask[0:96, hd % 2:hd % 2 + 1],
                                             None, ALU.mult)
                last.then_inc(kpad1_ready, 1)

            def sq(it, n, step):
                p, u = divmod(n, NU1)
                if u not in COMPLETE1:
                    return
                dve.wait_ge(Bh.act, drained(Bh, it, step, "s"))
                v = wts[:, p % 2, (u // 2 * 2) * S:(u + 1) * S]
                dve.tensor_scalar(v, v, 1.0, None, ALU.add).then_inc(plus1, 1)

            def den1(it, p, step):
                dve.wait_ge(den_done, it * NPAIR + p + 1)
                dve.transpose(d32[:, :], denB[:, :]).then_inc(den_read, 1)
                dve.wait_ge(den_read, it * NPAIR + p + 1)
                v = d32[:, :].rearrange("p (b c) -> p b c", c=32)
                part = rsplit[0:HD1, :].rearrange("p (b c) -> p b c", c=32)
                nb = P // 32
                chB.then(dve.tensor_copy(dlate[:, nb:], v[HD1:P, nb:, 0]))
                chB.then(dve.scalar_tensor_tensor(out=dsum[:, :], in0=v[0:HD1, :, 0], scalar=2 * TAYLOR_EPS,
                                                  in1=dlate[:, :], op0=ALU.add, op1=ALU.add))
                chB.then(dve.reciprocal(rrec[:, :], dsum[:, :]))
                chB.then(dve.tensor_copy(part[:, :, 0], rrec[:, :]))
                chB.then(dve.tensor_tensor(rrem[:, :], rrec[:, :], part[:, :, 0], ALU.subtract))
                chB.then(dve.tensor_copy(part[:, :, 1], rrem[:, :]))
                chB.then(dve.tensor_tensor(part[:, :, 2], rrem[:, :], part[:, :, 1], ALU.subtract))
                dve.transpose(rrows[:, :], rsplit[:, :]).then_inc(rrows_ready, 1)

            def scale(it, p, step):
                ps = full(dve, Bh, it, step, "r")
                dve.wait_ge(num_read, it * NPAIR + p + 1)
                dve.tensor_tensor(yT[:, p, :], ps[:, :], yT[:, p, :], ALU.mult).then_inc(Bh.dve, 1)

            def out1(it, n, step):
                ps = full(dve, Bh, it, step, "y")
                if n:
                    dve.wait_ge(Bh.dve, drained(Bh, it, f"out1 {n - 1}", "y"))
                dve.tensor_tensor(Bh.x[:, :, :].rearrange("p t d -> p (t d)"), ps[:, :],
                                  Bh.x[:, :, :].rearrange("p t d -> p (t d)"), ALU.add).then_inc(Bh.dve, 1)

            def start(it_of):
                for h, ch in (("A", chA), ("B", chB)):
                    if h in it_of:
                        ch.start(it_of[h])

            def end(it_of):
                for h, ch in (("A", chA), ("B", chB)):
                    if h in it_of:
                        ch.end()

            fns = dict(stat=stat, centre=centre, split=split, down0=down0, qkv0=qkv0, pad0=pad0, pv0=pv0, turn=turn,
                       out0=out0, take=take, route=route, gate=gate, expert=expert, qk1=qk1, v1=values1, pad1=pad1, sq=sq, den=den1,
                       scale=scale, out1=out1)
            fns["max"] = rowmax
            run(dve, fns, start, end)

        @block.tensor
        def _(pe):
            mm = nc.tensor.matmul
            pe.wait_ge(w_first, 16 * NW_FIRST)
            mm(ringA[0][:, :], U1T[:, :], V1[:, :], start=True, stop=True)
            for f in range(NF):
                last = mm(ringA[1][:, f * D:(f + 1) * D], U2T[:, f * P:(f + 1) * P], V2[:, :], start=True, stop=True)
            last.then_inc(lowrank, 1)
            pe.wait_ge(lowrank_copied, 2)
            pe.wait_ge(setup, SETUP)

            def norm(h, it, k, step):
                pe.wait_ge(h.ln_ready, it * h.lns + k + 1)
                ps = fill(pe, h, it, step, "lnT")
                for t in range(NT):
                    last = nc.tensor.transpose(ps[:, t * P:(t + 1) * P], h.ln[:, t, :], ident[:, :])
                last.then_inc(h.filled, 1)

            def split(it, k, step):
                norm(Bh, it, k, step)

            def of_tokens(out, weight, cols, tokens=slice(0, S), tokens_first=False):
                c0 = first_col[weight]
                for a, b, first, last in ((0, 0, True, False), (1, 0, False, False), (0, 1, False, True)):
                    wt = pairs[:, a, c0 + cols.start:c0 + cols.stop]
                    ln = (Bh.lnT_hi, Bh.lnT_lo)[b][:, tokens]
                    left, right = (ln, wt) if tokens_first else (wt, ln)
                    done = mm(out, left, right, start=first, stop=last)
                return done

            def up0(it, n, step):
                pe.wait_ge(A.act, drained(A, it, f"norm {(0, 3)[n // 2]}", "lnT"))
                for unit, _ in ring_uses(step):
                    f = int(unit[2:])
                    ps = fill(pe, A, it, step, unit)
                    mm(ps[:, :], w1[:, f * P:(f + 1) * P], A.lnT[:, :], start=True, stop=True).then_inc(A.filled, 1)

            def down0(it, n, step):
                first = n % 2 == 0
                ps = fill(pe, A, it, f"down0 {n + 1}" if first else step, "y")
                tiles = (0, 1) if first else (2, 3)
                pe.wait_ge(A.act, drained(A, it, f"up0 {n}", f"up{tiles[1]}"))
                for t in range(NT):
                    for f in tiles:
                        last = mm(ps[:, t * P:(t + 1) * P], hid0[:, f, t * P:(t + 1) * P], w2[:, f, :],
                                  start=f == 0 and t == 0, stop=f == NF - 1 and t == NT - 1)
                if not first:
                    last.then_inc(A.filled, 1)

            def qkv0(it, n, step):
                pe.wait_ge(w_rest, 16 * (NW - NW_FIRST))
                pe.wait_ge(tables, GH + 3)
                pe.wait_ge(A.act, drained(A, it, "norm 1", "lnT"))
                for name, wt in (("q", wq0), ("k", wk0)):
                    ps = fill(pe, A, it, step, name)
                    mm(ps[:, :], wt[:, :], A.lnT[:, :], start=True, stop=True).then_inc(A.filled, 1)
                ps = fill(pe, A, it, step, "v")
                for t in range(NT):
                    last = mm(ps[:, t * P:(t + 1) * P], A.lnT[:, t * P:(t + 1) * P], wv0[:, :], start=True, stop=True)
                last.then_inc(A.filled, 1)

            def rowmax(it, n, step):
                g, u = divmod(n, NU0)
                if u == 0:
                    pe.wait_ge(kpad0_ready, it * NG + g + 1)
                ps = fill(pe, A, it, step, "s")
                for kt, j in UNITS0[u]:
                    qt, c0 = NT - 1 - kt, segment(kt, j, GH) - u * S
                    n_keys = (qt + 1) * P
                    mm(ps[:, c0:c0 + n_keys], q0a[:, g, qt * P:(qt + 1) * P],
                       kpad0[:, g * GH + j, 0:n_keys], start=True, stop=False)
                    last = mm(ps[:, c0 + n_keys - P:c0 + n_keys], identb[:, :], negmask[:, :],
                              start=False, stop=True)
                last.then_inc(A.filled, 1)

            def shift(it, g, step):
                pe.wait_ge(rmax_ready, it * NG + g + 1)
                ps = fill(pe, A, it, step, "mT")
                for t in range(NT):
                    last = nc.tensor.transpose(ps[0:GH, t * P:(t + 1) * P], rmax[:, t, g * GH:(g + 1) * GH],
                                               ident[:, :])
                last.then_inc(A.filled, 1)

            def exp(it, n, step):
                g, u = divmod(n, NU0)
                if u == 0:
                    pe.wait_ge(offs_laid[g], (it + 1) * 16)
                ps = fill(pe, A, it, step, "s")
                for kt, j in UNITS0[u]:
                    c0 = segment(kt, j, GH) - u * S
                    last = mm(ps[:, c0:c0 + WIDTH[kt]], kpad0[:, g * GH + j, kt * P:(kt + 1) * P],
                              q0a[:, g, kt * P:S], start=True, stop=True)
                last.then_inc(A.filled, 1)

            def pv0(it, g, step):
                if g:
                    pe.wait_ge(oT_ready, it * NG + g)
                for i, kt in enumerate((0, 1, 3, 2)):
                    pe.wait_ge(masked0, it * NG * NT + g * NT + i + 1)
                    for j in range(GH):
                        c0 = segment(kt, j, GH)
                        last = mm(accA[VC * j:VC * j + HD0 + 1, kt * P:S], vaug[:, kt, g * GH + j, :],
                                  probs[:, g % 2, c0:c0 + WIDTH[kt]], start=kt == 0, stop=kt == 2)
                last.then_inc(pv0_done, 1)

            def turn(it, g, step):
                pe.wait_ge(oT_ready, it * NG + g + 1)
                ps = fill(pe, A, it, step, "o")
                for t in range(NT):
                    last = nc.tensor.transpose(ps[:, t * P:(t + 1) * P], oT[:, g % 2, t * P:(t + 1) * P], ident[:, :])
                last.then_inc(A.filled, 1)

            def out0(it, n, step):
                pe.wait_ge(A.act, drained(A, it, "norm 2", "lnT"))
                ps = fill(pe, A, it, step, "y")
                for t in range(NT):
                    last = mm(ps[:, t * P:(t + 1) * P], A.lnT[:, t * P:(t + 1) * P], wo0[:, :], start=True, stop=True)
                last.then_inc(A.filled, 1)

            def router(it, n, step):
                pe.wait_ge(w_split, 1)
                pe.wait_ge(Bh.dve, drained(Bh, it, f"split {(0, 2)[n]}", "lnT"))
                ps = fill(pe, Bh, it, step, "router")
                for t in range(NT):
                    last = of_tokens(ps[:, t * NE:(t + 1) * NE], "rw", slice(0, NE), slice(t * P, (t + 1) * P), True)
                last.then_inc(Bh.filled, 1)

            def gate(it, nf, step):
                f = nf % NS
                for unit, wt in (("gate", "sw1"), ("lin", "sw3")):
                    ps = fill(pe, Bh, it, step, unit)
                    of_tokens(ps[:, :], wt, slice(f * P, (f + 1) * P)).then_inc(Bh.filled, 1)

            def expert(it, ne, step):
                n, e = ne // NE, ne % NE
                first = (it * 2 + n) * (NE + 1)
                for unit, _ in ring_uses(step):
                    ps = fill(pe, Bh, it, step, unit)
                    k = int(unit[1:])
                    of_tokens(ps[:, :], "ew1", slice(k * HR, (k + 1) * HR)).then_inc(Bh.filled, 1)
                if e == 0:
                    pe.wait_ge(Bh.dve, drained(Bh, it, f"gate {n * NS + NS - 1}", "lin"))
                    for t in range(NT):
                        for f in range(NS):
                            last = mm(numB[:, t * P:(t + 1) * P], hsh[:, f, t * P:(t + 1) * P], sw2[:, f, :],
                                      start=f == 0, stop=f == NS - 1)
                    last.then_inc(moe_out, 1)
                else:
                    pe.wait_ge(moe_added, first + e)
                pe.wait_ge(Bh.act, drained(Bh, it, *unit_of_expert(n, e)))
                ps = (denB, numB)[e % 2]
                for t in range(NT):
                    last = mm(ps[:, t * P:(t + 1) * P], hexp[:, e % 2, t * P:(t + 1) * P], ew2[:, e, :],
                              start=True, stop=True)
                last.then_inc(moe_out, 1)

            def qk1(it, n, step):
                pe.wait_ge(Bh.dve, drained(Bh, it, "split 1", "lnT"))
                for name, wt in (("q", "wq1"), ("k", "wk1")):
                    for t in range(2):
                        ps = fill(pe, Bh, it, step, f"{name}{t}")
                        of_tokens(ps[:, :], wt, slice(t * P, (t + 1) * P)).then_inc(Bh.filled, 1)

            def values1(it, t, step):
                for c, unit in enumerate(("low", "high")):
                    ps = fill(pe, Bh, it, step, unit)
                    of_tokens(ps[:, :], "wv1", slice(c * S, (c + 1) * S), slice(t * P, (t + 1) * P), True)\
                        .then_inc(Bh.filled, 1)

            def sq(it, n, step):
                p, u = divmod(n, NU1)
                if p < 4 and u == 0:
                    pe.wait_ge(kpad1_ready, it * 4 + p + 1)
                ps = fill(pe, Bh, it, step, "s")
                for kt, j in UNITS1[u]:
                    c0 = segment(kt, j, 2) - u * S
                    last = mm(ps[:, c0:c0 + WIDTH[kt]], kpad1[:, 2 * p + j, kt * P:(kt + 1) * P],
                              q1a[:, p, kt * P:S], start=True, stop=True)
                last.then_inc(Bh.filled, 1)

            def den1(it, p, step):
                if p:
                    pe.wait_ge(den_read, it * NPAIR + p)
                late = {0: 0, 3: 0, 1: 1, 2: 1}
                for i, kts in enumerate(((0, 1), (3, 2))):
                    pe.wait_ge(masked1, (it * NPAIR + p) * NT + (2, 4)[i])
                    for kt in kts:
                        for j in range(2):
                            c0, row = segment(kt, j, 2), HD1 * late[kt] + 32 * j
                            last = mm(denB[row:row + 32, kt * P:S], ones[:, 0:32],
                                      wts[:, p % 2, c0:c0 + WIDTH[kt]], start=kt < 2, stop=kt >= 2)
                last.then_inc(den_done, 1)

            def num(it, p, step):
                if p:
                    pe.wait_ge(num_read, it * NPAIR + p)
                for kt in (0, 1, 3, 2):
                    for j in range(2):
                        c0, hd = segment(kt, j, 2), 2 * p + j
                        last = mm(numB[HD1 * j:HD1 * j + HD1, kt * P:S], v1[:, kt, hd * HD1:(hd + 1) * HD1],
                                  wts[:, p % 2, c0:c0 + WIDTH[kt]], start=kt == 0, stop=kt == 2)
                last.then_inc(pv1_done, 1)

            def scale(it, p, step):
                pe.wait_ge(rrows_ready, it * NPAIR + p + 1)
                ps = fill(pe, Bh, it, step, "r")
                mm(ps[:, :], spread[:, :], rrows[:, :], start=True, stop=True).then_inc(Bh.filled, 1)

            def out1(it, n, step):
                some = OUT1_PAIRS[n]
                pe.wait_ge(Bh.dve, drained(Bh, it, f"scale {some[-1]}", "r"))
                ps = fill(pe, Bh, it, step, "y")
                for t in range(NT):
                    for p in some:
                        last = mm(ps[:, t * P:(t + 1) * P], yT[:, p, t * P:(t + 1) * P], wo1[:, p, :],
                                  start=p == some[0], stop=p == some[-1])
                last.then_inc(Bh.filled, 1)

            fns = dict(norm=norm, split=split, up0=up0, down0=down0, qkv0=qkv0, shift=shift, exp=exp, pv0=pv0, turn=turn,
                       out0=out0, router=router, gate=gate, expert=expert, qk1=qk1, v1=values1, sq=sq, den=den1,
                       num=num, scale=scale, out1=out1)
            fns["max"] = rowmax
            run(pe, fns)


def kernel(**inputs):
    import concourse.bacc as _bacc
    from concourse.bass_utils import run_bass_kernel_spmd as _run

    a = {k: np.asarray(v) for k, v in inputs.items()}
    rows = lambda m: np.ascontiguousarray(m)
    tiles = lambda m: rows(m.reshape(-1, P, m.shape[-1]).transpose(1, 0, 2))
    wv0 = a["L0_attn_Wv"].reshape(HD0, H0, D).transpose(1, 0, 2).reshape(D, D)
    weights = {
        "U1T": rows(a["L0_ffn_U1"].T), "V1": rows(a["L0_ffn_V1"]), "U2T": rows(a["L0_ffn_U2"].T),
        "V2": rows(a["L0_ffn_V2"]), "b1": rows(a["L0_ffn_b1"].reshape(NF, P).T),
        "b2": rows(np.broadcast_to(a["L0_ffn_b2"], (P, NT, D))),
        "wq0": rows(a["L0_attn_Wq"].T), "wk0": rows(a["L0_attn_Wk"].T), "wv0": rows(wv0.T),
        "wo0": rows(a["L0_attn_Wo"].T), "gb": rows(np.stack([a["L0_attn_gamma"], a["L0_attn_beta"]], 1)),
        "wq1": rows(a["L1_attn_Wq"].T), "wk1": rows(a["L1_attn_Wk"].T), "wv1": rows(a["L1_attn_Wv"].T),
        "wo1": tiles(a["L1_attn_Wo"].T), "rw": rows(a["L1_ffn_router_w"].T),
        "rbias": rows(np.broadcast_to(a["L1_ffn_router_bias"], (P, NT, NE))),
        "sw1": rows(a["L1_ffn_sw1"]), "sw3": rows(a["L1_ffn_sw3"]), "sw2": tiles(a["L1_ffn_sw2"]),
        "ew1": rows(a["L1_ffn_ew1"].transpose(1, 0, 2).reshape(D, NE * HR)),
        "ew2": rows(a["L1_ffn_ew2"].transpose(1, 0, 2)),
    }
    p, q = np.arange(P)[:, None], np.arange(P)[None, :]
    j = np.arange(GH)[None, :]
    consts = {
        "ident": (p == q), "negmask": np.where(q > p, MASKED, 0.0),
        "headmask": np.where(p < OFF_ROW, (p % 32) // HD0 == j, (p == OFF_ROW + j) * OFF_UNIT),
        "spread": (p // 32 == q // HD1) & (p % 32 < 3),
        "pairmask": (p % 32) // FEAT == np.arange(2)[None, :],
        "iota8": np.broadcast_to(np.arange(NE), (P, NT, NE)),
    }
    consts = {k: np.ascontiguousarray(v, dtype=np.float32) for k, v in consts.items()}

    nc = _bacc.Bacc("TRN2", target_bir_lowering=False, num_devices=1)
    arrays = {"x_dram": rows(a["L0_attn_x"])}

    def dram(name, array):
        arrays[name] = array
        return nc.dram_tensor(name, array.shape, mybir.dt.from_np(array.dtype), kind="ExternalInput").ap()

    x_ap = dram("x_dram", arrays["x_dram"])
    w_aps = {k: dram(f"{k}_dram", v) for k, v in weights.items()}
    c_aps = {k: dram(f"{k}_const", v) for k, v in consts.items()}
    out_ap = nc.dram_tensor("out_dram", (B, S, D), F32, kind="ExternalOutput").ap()
    build_program(nc, x_ap, w_aps, c_aps, out_ap)
    r = _run(nc, [arrays], core_ids=[0])
    return r.results[0]["out_dram"]
```
